# Optimizing a Trainium2 kernel written in Bass

```python
import numpy as np
import jax
import jax.numpy as jnp

def _softmax(x, axis=-1):
    return jax.nn.softmax(x, axis=axis)

def _gelu(x):
    return jax.nn.gelu(x, approximate=True)

def _silu(x):
    return jax.nn.silu(x)

def _sigmoid(x):
    return jax.nn.sigmoid(x)

def _layernorm(x, axis=-1, eps=1e-05):
    m = jnp.mean(x, axis=axis, keepdims=True)
    v = jnp.var(x, axis=axis, keepdims=True)
    return (x - m) / jnp.sqrt(v + eps)

def _scatter_add(tgt, idx, src, axis=0):
    return tgt.at[idx].add(src)

def _segment_sum(src, seg, n):
    return jax.ops.segment_sum(src, seg, n)
kernel_name = 'mk_gnn_preln_d2_gnn_r32_1130ef'

def setup_inputs(seed: int=0):
    np.random.seed(seed)
    _w = jnp.asarray

    def _rec_inputs():
        import jax
        import jax.numpy as jnp
        _gk = jax.random.key(seed)
        x = -0.000202 + 1 * jax.random.normal(jax.random.fold_in(_gk, 1), (50000, 128), jnp.float32)
        src = jax.random.randint(jax.random.fold_in(_gk, 2), (25000,), 0, 50000, jnp.int32)
        dst = jnp.minimum((50000 * jax.random.uniform(jax.random.fold_in(_gk, 3), (25000,)) ** 2.0).astype(jnp.int32), 49999)
        _o = jnp.argsort(dst, stable=True)
        src = src[_o]
        dst = dst[_o]
        edge_type_8 = jax.random.randint(jax.random.fold_in(_gk, 13), (25000,), 0, 8, jnp.int32)
        return (x, src, dst, edge_type_8)
    x, src, dst, edge_type_8 = _rec_inputs()

    def _L0_gnn_setup():
        import jax, jax.numpy as jnp
        import numpy as np
        N = 50000
        E = 50000
        IN = 128
        OUT = 128
        H = 4
        HD = OUT // H
        key = jax.random.key(seed)
        k1, k2, k3, k4, k5 = jax.random.split(key, 5)
        x = jax.random.normal(k1, (N, IN), dtype=jnp.float32)
        edge_index = jax.random.randint(k2, (2, E), 0, N, dtype=jnp.int64)
        W = jax.random.normal(k3, (OUT, IN), dtype=jnp.float32) * (1.0 / np.sqrt(IN))
        att_src = jax.random.normal(k4, (1, H, HD), dtype=jnp.float32) * 0.1
        att_dst = jax.random.normal(k5, (1, H, HD), dtype=jnp.float32) * 0.1
        return {'x': x, 'edge_index': edge_index, 'W': W, 'att_src': att_src, 'att_dst': att_dst}
    _L0_gnn_all = _L0_gnn_setup()
    _L0_gnn_in = {k: v for k, v in _L0_gnn_all.items() if k in ('W', 'att_src', 'att_dst')}
    del _L0_gnn_all

    def _L1_gnn_setup():
        import jax, jax.numpy as jnp
        import numpy as np
        N_NODES = 3125
        N_EDGES = 25000
        D = 128
        L = 3
        R = 8
        B = 4
        key = jax.random.key(seed)
        ks = jax.random.split(key, 8)
        scale = (2.0 / D) ** 0.5
        feat = jax.random.normal(ks[0], (N_NODES, D), dtype=jnp.float32)
        basis = jax.random.normal(ks[1], (L, B, D, D), dtype=jnp.float32) * scale
        comb = jax.random.normal(ks[2], (L, R, B), dtype=jnp.float32) * 0.5
        w_loop = jax.random.normal(ks[3], (L, D, D), dtype=jnp.float32) * scale
        bias = jnp.zeros((L, D), dtype=jnp.float32)
        src = jax.random.randint(ks[4], (N_EDGES,), 0, N_NODES, dtype=jnp.int32)
        dst = jax.random.randint(ks[5], (N_EDGES,), 0, N_NODES, dtype=jnp.int32)
        etype = jax.random.randint(ks[6], (N_EDGES,), 0, R, dtype=jnp.int32)
        return {'feat': feat, 'basis': basis, 'comb': comb, 'w_loop': w_loop, 'bias': bias, 'src': src, 'dst': dst, 'etype': etype}
    _L1_gnn_all = _L1_gnn_setup()
    _L1_gnn_in = {k: v for k, v in _L1_gnn_all.items() if k in ('basis', 'comb', 'w_loop', 'bias')}
    del _L1_gnn_all
    return {'x': x, 'src': src, 'dst': dst, 'edge_type_8': edge_type_8, 'L0_gnn_W': _L0_gnn_in['W'], 'L0_gnn_att_src': _L0_gnn_in['att_src'], 'L0_gnn_att_dst': _L0_gnn_in['att_dst'], 'L1_gnn_basis': _L1_gnn_in['basis'], 'L1_gnn_comb': _L1_gnn_in['comb'], 'L1_gnn_w_loop': _L1_gnn_in['w_loop'], 'L1_gnn_bias': _L1_gnn_in['bias']}

def reference(x, src, dst, edge_type_8, L0_gnn_W, L0_gnn_att_src, L0_gnn_att_dst, L1_gnn_basis, L1_gnn_comb, L1_gnn_w_loop, L1_gnn_bias):
    import jax
    import jax.numpy as jnp

    def _L0_gnn_ref(x, edge_index, W, att_src, att_dst):
        import jax, jax.numpy as jnp
        import numpy as np
        N = 50000
        E = 50000
        IN = 128
        OUT = 128
        H = 4
        HD = OUT // H
        n = x.shape[0]
        loops = jnp.arange(n, dtype=edge_index.dtype)
        ei = jnp.concatenate([edge_index, jnp.stack([loops, loops])], axis=1)
        src, dst = (ei[0], ei[1])
        h = (x @ W.T).reshape(n, H, HD)
        a_src = jnp.sum(h * att_src, axis=-1)
        a_dst = jnp.sum(h * att_dst, axis=-1)
        alpha = a_src[src] + a_dst[dst]
        alpha = jax.nn.leaky_relu(alpha, negative_slope=0.2)
        m = jax.ops.segment_max(alpha, dst, num_segments=n)
        e = jnp.exp(alpha - m[dst])
        s = jax.ops.segment_sum(e, dst, num_segments=n)
        e = e / s[dst]
        msg = h[src] * (e[:, :, None] + 1.0)
        out = jax.ops.segment_sum(msg, dst, num_segments=n)
        return out.reshape(n, -1)

    def _L1_gnn_ref(feat, basis, comb, w_loop, bias, src, dst, etype):
        import jax, jax.numpy as jnp
        import numpy as np
        N_NODES = 3125
        N_EDGES = 25000
        D = 128
        L = 3
        R = 8
        B = 4
        n = feat.shape[0]
        h = feat
        for l in range(basis.shape[0]):
            W = jnp.einsum('rb,bio->rio', comb[l], basis[l])
            proj = jnp.einsum('ni,rio->rno', h, W)
            msg = proj[etype, src]
            agg = jax.ops.segment_sum(msg, dst, num_segments=n)
            out = agg + h @ w_loop[l] + bias[l]
            h = jax.nn.relu(out) + h
        return h
    edge_index = jnp.stack([src, dst])
    h = jnp.maximum(_layernorm(x, axis=-1), 0.0)
    x = x + _L0_gnn_ref(h, edge_index, L0_gnn_W, L0_gnn_att_src, L0_gnn_att_dst)
    h = jnp.maximum(_layernorm(x, axis=-1), 0.0)
    x = x + _L1_gnn_ref(h, L1_gnn_basis, L1_gnn_comb, L1_gnn_w_loop, L1_gnn_bias, src, dst, edge_type_8)
    return x

_drawn_inputs = setup_inputs


def setup_inputs(seed=0):
    import zlib

    import numpy as np

    out = dict(_drawn_inputs(seed))
    spreads = {'L1_gnn_bias': (0.0, 0.1)}
    factors = {'L0_gnn_att_src': 3.802, 'L0_gnn_att_dst': 8.0}
    for name, (base, spread) in spreads.items():
        noise = np.random.default_rng([zlib.crc32(name.encode()), seed]).standard_normal(out[name].shape)
        drawn = base * np.exp(spread * noise) if base else spread * noise
        out[name] = jnp.asarray(drawn.astype(out[name].dtype))
    for name, factor in factors.items():
        out[name] = (out[name] * factor).astype(out[name].dtype)
    return out
```

```python
import numpy as np
import concourse.bass as bass
from concourse import mybir
from contextlib import ExitStack

N, D, E = 50000, 128, 25000
HEADS, HD = 4, 32
REL, BASES, LAYERS = 8, 4, 3
P = 128
TE = P - 1
G = 3
UG = 2 * G
TURNS = -(-E // (TE * UG))
NT = TURNS * UG
SLOTS = NT * P
J = 4
UNIT = P * J
UNITS = -(-N // UNIT)
LAST_UNIT = N - UNIT
NODE_TURNS = UNITS // 2
BLOCKS = -(-NT // 32)
PLACE_COLS = -(-N // P)
NO_EDGE, NO_SEGMENT = N, N + 1
SKIP = 65536
BIG = 1.0e30
EPS = 1e-5
SLOPE = 0.2
W0 = D + 2 * HEADS
SEG = 2 * D + HEADS
CONSTS = 18
assert UNITS % 2 == 0 and NT * TE >= E


class Order:

    def __init__(self, eng, sem):
        self.eng, self.sem, self.base, self.k = eng, sem, 0, 0

    def mark(self, ins):
        ins.then_inc(self.sem, 1)
        self.k += 1

    def wait(self):
        self.eng.wait_ge(self.sem, self.base + self.k)


def turns(eng, body, n, order=None):
    start = 0
    if order:
        start, order.k, order.base = order.base + order.k, 0, order.base + order.k
    body(0)
    per = order.k if order else 0
    with eng.Fori(1, n - 1) as i:
        if order:
            order.base, order.k = start + i * per, 0
        body(i)
    if order:
        order.base, order.k = start + (n - 1) * per, 0
    body(n - 1)


def wait(eng, sem, value):
    if not (isinstance(value, int) and value <= 0):
        eng.wait_ge(sem, value)


def program(nc, x, src, dst_cols, col_dst, next_dst, dst_gather, etype, scan_dst, tile_ends, consts, W, att,
            basis, comb, w_loop, bias, out):
    fp32, i32 = mybir.dt.float32, mybir.dt.int32
    ALU, ACT, AX = mybir.AluOpType, mybir.ActivationFunctionType, mybir.AxisListType

    with ExitStack() as ctx:
        def sb(name, shape, dt=fp32):
            return ctx.enter_context(nc.sbuf_tensor(name, shape, dt))

        def sem(name):
            return ctx.enter_context(nc.semaphore(name))

        def dram(name, shape, dt=fp32):
            return nc.dram_tensor(name, shape, dt, kind="Internal").ap()

        h_tab = [dram(f"h_tab{l}", (N + SLOTS, D)) for l in range(LAYERS)]
        ident = sb("ident", [P, P])
        headmask = sb("headmask", [P, HEADS])
        w_rows = sb("w_rows", [P, D])
        att_cols = sb("att_cols", [P, 2])
        att_mat = sb("att_mat", [P, 2 * HEADS])
        w0 = sb("w0", [P, W0])
        wl = sb("wl", [P, LAYERS, D])
        basis_sb = sb("basis_sb", [P, LAYERS, BASES * D])
        bias_row = sb("bias_row", [P, LAYERS, D])
        bias_col = sb("bias_col", [P, LAYERS])
        eps = sb("eps", [P, 1])
        zeros = sb("zeros", [1, SEG])

        banks = ctx.enter_context(nc.psum_tensor("banks", [P, 8, 512], fp32))
        psum = [banks[:, b, :] for b in range(8)]

        s_const = sem("s_const")
        s_order = sem("s_order")
        s_setup = sem("s_setup")
        s_wt = sem("s_wt")
        s_w0 = sem("s_w0")
        s_phase = sem("s_phase")

        xn = [sb(f"xn{v}", [P, J, D]) for v in range(2)]
        x1n = [sb(f"x1n{v}", [P, J, D]) for v in range(2)]
        h0n = [sb(f"h0n{v}", [P, J, D]) for v in range(2)]
        h1n = [sb(f"h1n{v}", [P, J, D]) for v in range(2)]
        h2n = [sb(f"h2n{v}", [P, J, D]) for v in range(2)]
        on = [sb(f"on{v}", [P, J, D]) for v in range(2)]
        hn = sb("hn", [P, J, D])
        hnT = sb("hnT", [P, UNIT])
        hT = [sb(f"hT{l}", [P, UNIT]) for l in range(LAYERS + 1)]
        rT = [sb(f"rT{l}", [P, UNIT]) for l in range(LAYERS)]
        stats = sb("stats", [P, 2 * G, 6])
        lnt = sb("lnt", [P, 5, 2 * G])
        std = sb("std", [P, 2 * G])
        rstd = sb("rstd", [P, 2 * G])
        shift = sb("shift", [P, 2 * G])

        n_x = [sem(f"n_xload{v}") for v in range(2)]
        n_var1, n_std1, n_rs1 = sem("n_var1"), sem("n_std1"), sem("n_rs1")
        n_h = sem("n_h")
        n_t = sem("n_t")
        n_ht = sem("n_ht")
        n_m = sem("n_m")
        n_x1 = sem("n_x1")
        n_var2, n_std2, n_rs2 = sem("n_var2"), sem("n_std2"), sem("n_rs2")
        n_h0 = sem("n_h0")
        n_t0, n_h0t = sem("n_t0"), sem("n_h0t")
        n_z = [sem(f"n_z{l}") for l in range(LAYERS)]
        n_r = [sem(f"n_r{l}") for l in range(LAYERS)]
        n_a = [sem(f"n_a{l}") for l in range(LAYERS)]
        n_tb = [sem(f"n_tb{l}") for l in range(LAYERS)]
        n_rows = [sem(f"n_rows{l}") for l in range(2)]
        n_out = sem("n_out")
        n_st = [[sem(f"n_st{k}_{v}") for v in range(2)] for k in range(4)]

        place_tab = dram("place_tab", (PLACE_COLS * P, 1), i32)
        l0_tab = dram("l0_tab", (SLOTS, 3 * D))
        same_tab = dram("same_tab", (SLOTS, P))
        x1_tab = dram("x1_tab", (SLOTS, D))
        src_i, dstg_i, dst_i, next_i, etype_i = (sb(n_, [P, NT], i32) for n_ in
                                                 ("src_i", "dstg_i", "dst_i", "next_i", "etype_i"))
        dst_f = sb("dst_f", [P, NT])
        is_r = sb("is_r", [P, REL, NT])
        repeat_f = sb("repeat_f", [P, NT])
        last_idx = sb("last_idx", [P, NT], i32)
        slot_row = sb("slot_row", [P, NT], i32)
        src_row = sb("src_row", [P, NT], i32)
        place_init = sb("place_init", [P, PLACE_COLS], i32)
        comb_bc = sb("comb_bc", [P, LAYERS, REL, BASES])
        coef = sb("coef", [P, LAYERS, NT, BASES])
        pool_idx = [sb(f"pool_idx{u}", [P, 2 * G], i32) for u in range(2)]
        pool_val = [sb(f"pool_val{u}", [P, G], i32) for u in range(2)]
        headsel = sb("headsel", [P, P])
        tilesel = sb("tilesel", [P, 32])
        logit = sb("logit", [P, BLOCKS * 32 * HEADS])
        own = sb("own", [P, NT * HEADS])
        top = sb("top", [P, NT * HEADS])
        scan_i = sb("scan_i", [P, BLOCKS, P], i32)
        ends_i = sb("ends_i", [P, 2, BLOCKS * 32], i32)
        ends_f = sb("ends_f", [P, BLOCKS, 2])
        best, differ, up, down = (sb(n_, [P, BLOCKS, P]) for n_ in ("best", "differ", "up", "down"))
        edge_max = sb("edge_max", [P, 2, BLOCKS, 32])
        pick = sb("pick", [P, BLOCKS, BLOCKS * 32])
        beyond = sb("beyond", [P, 2, BLOCKS])

        xg = [sb(f"xg{u}", [P, 2, G, D]) for u in range(2)]
        ah = [sb(f"ah{u}", [P, 2 * G, D]) for u in range(2)]
        ahT = [sb(f"ahT{u}", [P, 2 * G, P]) for u in range(2)]
        e0 = [sb(f"e0{u}", [P, 2, G, W0]) for u in range(2)]
        col_i = [sb(f"col_i{u}", [P, G, P], i32) for u in range(2)]
        same = [sb(f"same{u}", [P, G, P]) for u in range(2)]
        l0 = [sb(f"l0{u}", [P, G, 3 * D]) for u in range(2)]
        msg0 = [sb(f"msg0{u}", [P, G, SEG]) for u in range(2)]
        den, rden, pself = (sb(n_, [P, G, HEADS]) for n_ in ("den", "rden", "pself"))
        t_nbr, t_own = sb("t_nbr", [P, G, D]), sb("t_own", [P, G, D])
        x1e = [sb(f"x1e{u}", [P, G, D]) for u in range(2)]
        hdst = [sb(f"hdst{u}", [P, G, D]) for u in range(2)]
        hnew = [sb(f"hnew{u}", [P, G, D]) for u in range(2)]
        hsrc = [sb(f"hsrc{u}", [P, G, D]) for u in range(2)]
        pairT = [sb(f"pairT{k}", [P, 2 * P]) for k in range(3)]
        msg = [sb(f"msg{k}", [P, D]) for k in range(2)]
        zsum = sb("zsum", [P, G, D])

        s_pool = sem("s_pool")
        s_iota = sem("s_iota")
        s_tab = sem("s_tab")
        s_idx = sem("s_idx")
        p_copy = sem("p_copy")
        p_sc = [sem(f"p_sc{u}") for u in range(2)]
        p_ga = [sem(f"p_ga{u}") for u in range(2)]
        p_row = sem("p_row")
        a_x = [sem(f"a_x{u}") for u in range(2)]
        a_col = [sem(f"a_col{u}") for u in range(2)]
        a_var, a_std, a_rs, a_h, a_t, a_ht, a_m, a_e0, a_al, a_same = (sem("a_" + n_) for n_ in
            ("var", "std", "rs", "h", "t", "ht", "m", "e0", "al", "same"))
        a_st = [sem(f"a_st{u}") for u in range(2)]
        m_t, m_pe, m_exp = sem("m_t"), sem("m_pe"), sem("m_exp")
        b_ld = [sem(f"b_ld{u}") for u in range(2)]
        b_st = [sem(f"b_st{u}") for u in range(2)]
        b_plain, b_msg, b_carry, b_seg, b_x1, b_var, b_std, b_rs, b_h = (sem("b_" + n_) for n_ in
            ("plain", "msg", "carry", "seg", "x1", "var", "std", "rs", "h"))
        e_ld = [sem(f"e_ld{u}") for u in range(2)]
        e_x1 = [sem(f"e_x1{u}") for u in range(2)]
        e_hs = [sem(f"e_hs{u}") for u in range(2)]
        e_st = [sem(f"e_st{u}") for u in range(2)]
        e_sc = [sem(f"e_sc{u}") for u in range(2)]
        e_t, e_ct, e_y, e_msg, e_carry, e_seg, e_out = (sem("e_" + n_) for n_ in
            ("t", "ct", "y", "msg", "carry", "seg", "out"))

        block = ctx.enter_context(nc.Block())

        def slot_rows(table, g, first=0, lo=0, hi=None):
            t = table[bass.ds(first + g * (G * P), G * P), lo:hi] if hi else table[bass.ds(first + g * (G * P), G * P), :]
            return t.rearrange("(j p) f -> p j f", p=P)

        def heads(ap):
            return ap.rearrange("p g (h d) -> p g h d", h=HEADS)

        def per_head(ap):
            return ap.unsqueeze(3).broadcast_to([P, G, HEADS, HD])

        def unit_rows(table, u):
            first = u * UNIT if not (isinstance(u, int) and u == UNITS - 1) else LAST_UNIT
            return table[bass.ds(first, UNIT), :].rearrange("(p j) f -> p j f", j=J)

        def phase_end(eng, k):
            eng.drain().then_inc(s_phase, 1)
            eng.wait_ge(s_phase, 4 * k)

        def ln_small(dve, order, n, s_std, std_count, s_var, s_rs):
            st = stats[:, 0:n, :]
            total, half, m2, sq, var = (lnt[:, c, 0:n] for c in range(5))
            order.wait()
            order.mark(nc.vector.tensor_tensor(total, st[:, :, 1], st[:, :, 4], ALU.add))
            order.mark(nc.vector.tensor_tensor(half, st[:, :, 1], st[:, :, 4], ALU.subtract))
            order.mark(nc.vector.tensor_tensor(m2, st[:, :, 2], st[:, :, 5], ALU.add))
            order.wait()
            order.mark(nc.vector.tensor_tensor(sq, half, half, ALU.mult))
            order.wait()
            nc.vector.scalar_tensor_tensor(out=var, in0=sq, scalar=D / 4.0, in1=m2, op0=ALU.mult,
                                           op1=ALU.add).then_inc(s_var, 1)

        def ln_scale(dve, order, n, s_std, std_count, s_rs):
            dve.wait_ge(s_std, std_count)
            order.mark(nc.vector.reciprocal(rstd[:, 0:n], std[:, 0:n]))
            order.wait()
            nc.vector.scalar_tensor_tensor(out=shift[:, 0:n], in0=lnt[:, 0, 0:n], scalar=-0.5, in1=rstd[:, 0:n],
                                           op0=ALU.mult, op1=ALU.mult).then_inc(s_rs, 1)

        def node_stream(eng, body_of, order=None):
            body_of(0, 0, 0, None, None, None)

            def body(i):
                for v in range(2):
                    u = 2 * i + v
                    more = not (isinstance(u, int) and u + 1 >= UNITS)
                    body_of(u + 1 if more else None, 1 - v, i + v, u, v, i)
            turns(eng, body, NODE_TURNS, order)

        @block.sync
        def _(sp):
            c = P + HEADS
            for dst_, src_ in (
                               (headsel[:, :], consts[:, c:c + P]), (tilesel[:, :], consts[:, c + P:c + P + 32]),
                               (src_i[:, :], src), (dstg_i[:, :], dst_gather), (dst_i[:, :], dst_cols),
                               (next_i[:, :], next_dst), (etype_i[:, :], etype),
                               (comb_bc[:, :, :, :], comb.partition_broadcast(P)),
                               (scan_i[:, :, :], scan_dst.rearrange("p (b c) -> p b c", b=BLOCKS)),
                               (ends_i[:, :, :], tile_ends.partition_broadcast(P)),
                               (ident[:, :], consts[:, 0:P]), (headmask[:, :], consts[:, P:P + HEADS]),
                               (w_rows[:, :], W), (att_cols[:, :], att),
                               (wl[:, :, :], w_loop.rearrange("l i o -> i l o")),
                               (basis_sb[:, :, :].rearrange("p l (b o) -> p l b o", b=BASES), basis.rearrange("l b i o -> i l b o")),
                               (bias_row[:, :, :], bias.partition_broadcast(P)),
                               (bias_col[:, :], bias.rearrange("l o -> o l"))):
                with nc.allow_non_contiguous_dma(reason="a few small constants"):
                    sp.dma_start(dst_, src_).then_inc(s_const, 16)

            def load(u, v, k):
                if not (isinstance(u, int) and u < 2):
                    sp.wait_ge(n_x1, u - 1)
                sp.dma_start(xn[v][:, :, :], unit_rows(x, u)).then_inc(n_x[v], 16)

            def store(u, v, i):
                last = isinstance(u, int) and u == UNITS - 1
                if last:
                    for k in range(4):
                        sp.wait_ge(n_st[k][1 - v], 16 * (i + 1))
                for k, (ready, rows, table) in enumerate(((n_h0, h0n, h_tab[0]), (n_rows[0], h1n, h_tab[1]),
                                                          (n_rows[1], h2n, h_tab[2]), (n_out, on, out))):
                    sp.wait_ge(ready, u + 1)
                    sp.dma_start(unit_rows(table, u), rows[v][:, :, :]).then_inc(n_st[k][v], 16)

            load(0, 0, 0)

            def body(i):
                for v in range(2):
                    u = 2 * i + v
                    if not (isinstance(u, int) and u + 1 >= UNITS):
                        load(u + 1, 1 - v, i)
                    store(u, v, i)
            turns(sp, body, NODE_TURNS)
            for k in range(4):
                for v in range(2):
                    sp.wait_ge(n_st[k][v], 16 * NODE_TURNS)
            phase_end(sp, 1)

            def a_load(g, u):
                wait(sp, a_same, g - 1)
                sp.dma_start(col_i[u][:, :, :].rearrange("p j c -> p (j c)"),
                             col_dst.rearrange("t c -> (t c)")[bass.ds(g * (G * P), G * P)].partition_broadcast(P))\
                    .then_inc(a_col[u], 16)

            def a_body(i):
                for u in range(2):
                    g = 2 * i + u
                    if not (isinstance(g, int) and g + 1 >= 2 * TURNS):
                        a_load(g + 1, 1 - u)
                    sp.wait_ge(a_same, g + 1)
                    sp.dma_start(slot_rows(same_tab, g), same[u][:, :, :]).then_inc(a_st[u], 16)
                    sp.wait_ge(a_e0, g + 1)
                    for k in range(2):
                        sp.dma_start(slot_rows(l0_tab, g, lo=k * D, hi=(k + 1) * D), e0[u][:, k, :, 0:D]).then_inc(a_st[u], 16)
                    sp.dma_start(slot_rows(l0_tab, g, lo=2 * D, hi=3 * D), xg[u][:, 1, :, :]).then_inc(a_st[u], 16)
            a_load(0, 0)
            turns(sp, a_body, TURNS)
            for u in range(2):
                sp.wait_ge(a_st[u], 64 * TURNS)
            phase_end(sp, 2)

            def b_load(g, u):
                wait(sp, b_x1, g - 1)
                sp.dma_start(l0[u][:, :, :], slot_rows(l0_tab, g)).then_inc(b_ld[u], 16)
                sp.dma_start(same[u][:, :, :], slot_rows(same_tab, g)).then_inc(b_ld[u], 16)

            def b_body(i):
                for u in range(2):
                    g = 2 * i + u
                    if not (isinstance(g, int) and g + 1 >= 2 * TURNS):
                        b_load(g + 1, 1 - u)
                    sp.wait_ge(b_x1, g + 1)
                    sp.dma_start(slot_rows(x1_tab, g), x1e[u][:, :, :]).then_inc(b_st[u], 16)
                    sp.wait_ge(b_h, g + 1)
                    sp.dma_start(slot_rows(h_tab[0], g, N), hnew[u][:, :, :]).then_inc(b_st[u], 16)
            b_load(0, 0)
            turns(sp, b_body, TURNS)
            for u in range(2):
                sp.wait_ge(b_st[u], 32 * TURNS)
            phase_end(sp, 3)

            for l in range(LAYERS):
                def e_load(g, u, l=l):
                    wait(sp, e_out, 2 * TURNS * l + g - 1)
                    sp.dma_start(hdst[u][:, :, :], slot_rows(h_tab[l], g, N)).then_inc(e_ld[u], 16)
                    sp.dma_start(same[u][:, :, :], slot_rows(same_tab, g)).then_inc(e_ld[u], 16)
                    if l == LAYERS - 1:
                        sp.dma_start(x1e[u][:, :, :], slot_rows(x1_tab, g)).then_inc(e_x1[u], 16)

                def e_body(i, l=l):
                    for u in range(2):
                        g = 2 * i + u
                        if not (isinstance(g, int) and g + 1 >= 2 * TURNS):
                            e_load(g + 1, 1 - u)
                        if l < LAYERS - 1:
                            sp.wait_ge(e_out, 2 * TURNS * l + g + 1)
                            sp.dma_start(slot_rows(h_tab[l + 1], g, N), hnew[u][:, :, :]).then_inc(e_st[u], 16)
                e_load(0, 0)
                turns(sp, e_body, TURNS)
                if l < LAYERS - 1:
                    for u in range(2):
                        sp.wait_ge(e_st[u], 16 * TURNS * (l + 1))
                phase_end(sp, 4 + l)

        @block.gpsimd
        def _(pool):
            order = Order(pool, p_copy)

            def pool_wait(s, value):
                if isinstance(value, int) and value <= 0:
                    return
                pool.wait_ge(s, value)
                pool.sem_inc(s_pool, 1)

            def copies(u, g, *pairs):
                for to, table in pairs:
                    ins = nc.gpsimd.tensor_copy(to, table[:, bass.ds(g * G, G)])
                    order.mark(ins)
                pool_wait(p_copy, order.base + order.k)

            nc.gpsimd.iota(place_init[:, :], [[1, PLACE_COLS]], base=0, channel_multiplier=PLACE_COLS).then_inc(s_iota, 1)
            nc.gpsimd.iota(slot_row[:, :], [[P, NT]], base=N, channel_multiplier=1).then_inc(s_iota, 1)
            pool.wait_ge(s_iota, 2)
            pool.dma_start(place_tab.rearrange("(p c) o -> p (c o)", p=P), place_init[:, :]).then_inc(s_tab, 16)
            pool.wait_ge(s_tab, 16)
            pool.wait_ge(s_idx, 1)

            def scatter_place(i):
                for u in range(2):
                    pool_wait(p_sc[u], 16 * G * i)
                    copies(u, 2 * i + u, (pool_idx[u][:, 0:G], last_idx), (pool_val[u][:, :], slot_row))
                    for j in range(G):
                        nc.gpsimd.indirect_dma_start(
                            out=place_tab, out_offset=bass.IndirectOffsetOnAxis(ap=pool_idx[u][:, j:j + 1], axis=0),
                            in_=pool_val[u][:, j:j + 1], in_offset=None, bounds_check=N - 1, oob_is_err=False).then_inc(p_sc[u], 16)
            turns(pool, scatter_place, TURNS, order)
            for u in range(2):
                pool.wait_ge(p_sc[u], 16 * G * TURNS)

            def gather_place(i):
                for u in range(2):
                    g = 2 * i + u
                    copies(u, g, (pool_idx[u][:, 0:G], src_i))
                    for j in range(G):
                        nc.gpsimd.indirect_dma_start(
                            out=pool_val[u][:, j:j + 1], out_offset=None, in_=place_tab,
                            in_offset=bass.IndirectOffsetOnAxis(ap=pool_idx[u][:, j:j + 1], axis=0)).then_inc(p_ga[u], 16)
                for u in range(2):
                    pool_wait(p_ga[u], 16 * G * (i + 1))
                    order.mark(nc.gpsimd.tensor_copy(src_row[:, bass.ds((2 * i + u) * G, G)], pool_val[u][:, :]))
            turns(pool, gather_place, TURNS, order)

            def gather_x(i):
                for u in range(2):
                    g = 2 * i + u
                    pool_wait(a_st[u], 64 * i)
                    copies(u, g, (pool_idx[u][:, 0:G], src_i), (pool_idx[u][:, G:2 * G], dstg_i))
                    for k in range(2):
                        for j in range(G):
                            nc.gpsimd.indirect_dma_start(
                                out=xg[u][:, k, j, :], out_offset=None, in_=x,
                                in_offset=bass.IndirectOffsetOnAxis(ap=pool_idx[u][:, k * G + j:k * G + j + 1], axis=0))\
                                .then_inc(a_x[u], 16)
            turns(pool, gather_x, TURNS, order)

            for l in range(LAYERS):
                pool.wait_ge(s_phase, 4 * (3 + l))

                def gather_h(g, u, l=l):
                    pool_wait(e_t, NT * l + G * (g - 1))
                    copies(u, g, (pool_idx[u][:, 0:G], src_row))
                    for j in range(G):
                        nc.gpsimd.indirect_dma_start(
                            out=hsrc[u][:, j, :], out_offset=None, in_=h_tab[l],
                            in_offset=bass.IndirectOffsetOnAxis(ap=pool_idx[u][:, j:j + 1], axis=0)).then_inc(e_hs[u], 16)

                def layer_turn(i, l=l):
                    for u in range(2):
                        g = 2 * i + u
                        if not (isinstance(g, int) and g + 1 >= 2 * TURNS):
                            gather_h(g + 1, 1 - u)
                        if l == LAYERS - 1:
                            pool_wait(e_sc[u], 16 * G * i)
                            copies(u, g, (pool_val[u][:, :], last_idx))
                            pool_wait(e_out, 2 * TURNS * l + g + 1)
                            for j in range(G):
                                nc.gpsimd.indirect_dma_start(
                                    out=out, out_offset=bass.IndirectOffsetOnAxis(ap=pool_val[u][:, j:j + 1], axis=0),
                                    in_=hnew[u][:, j, :], in_offset=None, bounds_check=N - 1, oob_is_err=False).then_inc(e_sc[u], 16)
                gather_h(0, 0)
                turns(pool, layer_turn, TURNS, order)
            for u in range(2):
                pool.wait_ge(e_sc[u], 16 * G * TURNS)

        @block.scalar
        def _(act):
            act.wait_ge(s_setup, 1)

            def relu_rows(out_rows, in_rows, n):
                for j in range(n):
                    last = nc.scalar.activation(out_rows[:, j, :], in_rows[:, j, :], ACT.Relu,
                                                bias=shift[:, j:j + 1], scale=rstd[:, j:j + 1])
                return last

            def root(s_var, count, s_std, n):
                act.wait_ge(s_var, count)
                nc.scalar.activation(std[:, 0:n], lnt[:, 4, 0:n], ACT.Sqrt, bias=eps[:, :], scale=1.0 / D).then_inc(s_std, 1)

            def first(u, v, i, step):
                if step == 0:
                    root(n_var1, u + 1, n_std1, J)
                elif step == 1:
                    act.wait_ge(n_rs1, u + 1)
                    relu_rows(hn, xn[v], J).then_inc(n_h, 1)
                elif step == 2:
                    act.wait_ge(n_t, u + 1)
                    nc.scalar.copy(hnT[:, :], psum[1][:, :]).then_inc(n_ht, 1)
                elif step == 3:
                    root(n_var2, u + 1, n_std2, J)
                elif step == 4:
                    act.wait_ge(n_rs2, u + 1)
                    wait(act, n_st[0][v], 16 * i)
                    relu_rows(h0n[v], x1n[v], J).then_inc(n_h0, 1)

            def relu_bias(u, l, bank):
                act.wait_ge(n_z[l], u + 1)
                nc.scalar.activation(rT[l][:, :], psum[bank][:, :], ACT.Relu, bias=bias_col[:, l:l + 1]).then_inc(n_r[l], 1)

            def rows(u, v, i, l, bank, to):
                act.wait_ge(n_tb[l], u + 1)
                wait(act, n_st[1 + l][v], 16 * i)
                nc.scalar.copy(to[v][:, :, :].rearrange("p j f -> p (j f)"), psum[bank][:, :]).then_inc(n_rows[l], 1)

            def body_of(u1, v1, i1, u2, v2, i2):
                if u1 is not None:
                    first(u1, v1, i1, 0)
                if u2 is not None:
                    act.wait_ge(n_t0, u2 + 1)
                    nc.scalar.copy(hT[0][:, :], psum[0][:, :]).then_inc(n_h0t, 1)
                if u1 is not None:
                    first(u1, v1, i1, 1)
                if u2 is not None:
                    relu_bias(u2, 0, 2)
                if u1 is not None:
                    first(u1, v1, i1, 2)
                if u2 is not None:
                    relu_bias(u2, 1, 5)
                if u1 is not None:
                    first(u1, v1, i1, 3)
                if u2 is not None:
                    rows(u2, v2, i2, 0, 4, h1n)
                if u1 is not None:
                    first(u1, v1, i1, 4)
                if u2 is not None:
                    relu_bias(u2, 2, 2)
                    rows(u2, v2, i2, 1, 6, h2n)

            node_stream(act, body_of)
            phase_end(act, 1)

            def a_body(i):
                for u in range(2):
                    g = 2 * i + u
                    root(a_var, g + 1, a_std, 2 * G)
                    wait(act, a_t, g - 1)
                    act.wait_ge(a_rs, g + 1)
                    relu_rows(ah[u], xg[u][:, :, :, :].rearrange("p k j f -> p (k j) f"), 2 * G).then_inc(a_h, 1)
                    act.wait_ge(a_t, g + 1)
                    for k in range(2):
                        last = nc.scalar.copy(ahT[u][:, k * G:(k + 1) * G, :].rearrange("p j f -> p (j f)"),
                                              psum[2 * u + k][:, 0:G * P])
                    last.then_inc(a_ht, 1)
                    act.wait_ge(a_m, g + 1)
                    wait(act, a_st[u], 64 * i)
                    wait(act, a_al, g - 1)
                    for k in range(2):
                        last = nc.scalar.copy(e0[u][:, k, :, :].rearrange("p j f -> p (j f)"), psum[4 + 2 * u + k][:, 0:G * W0])
                    last.then_inc(a_e0, 1)
            turns(act, a_body, TURNS)
            phase_end(act, 2)

            act.wait_ge(m_t, 7)
            nc.scalar.activation(logit[:, 0:NT * HEADS], logit[:, 0:NT * HEADS], ACT.Exp)
            nc.scalar.activation(own[:, :], own[:, :], ACT.Exp).then_inc(m_exp, 1)

            def plain(g, u, i):
                act.wait_ge(b_ld[u], 32 * (i + 1))
                wait(act, b_seg, G * (g - 1))
                nc.scalar.copy(msg0[u][:, :, D:2 * D], l0[u][:, :, 0:D]).then_inc(b_plain, 1)
                act.wait_ge(b_msg, g + 1)
                act.wait_ge(b_plain, g + 1)

            def carry(g, u, j):
                if j == 0 and isinstance(g, int) and g == 0:
                    held = zeros[:, :]
                else:
                    act.wait_ge(b_seg, G * g + j)
                    held = psum[(G * u + j - 1) % UG][0:1, 0:SEG]
                nc.scalar.copy(msg0[u][0:1, j, :], held).then_inc(b_carry, 1)

            def b_body(i):
                for u in range(2):
                    g = 2 * i + u
                    for j in range(1, G):
                        carry(g, u, j)
                    if not (isinstance(g, int) and g + 1 >= 2 * TURNS):
                        plain(g + 1, 1 - u, i + u)
                        carry(g + 1, 1 - u, 0)
                    root(b_var, g + 1, b_std, G)
                    act.wait_ge(b_rs, g + 1)
                    wait(act, b_st[u], 32 * i)
                    relu_rows(hnew[u], x1e[u], G).then_inc(b_h, 1)
            plain(0, 0, 0)
            carry(0, 0, 0)
            turns(act, b_body, TURNS)
            phase_end(act, 3)

            for l in range(LAYERS):
                def turned(i, j, l=l):
                    i, j = i + j // UG, j % UG
                    if isinstance(i, int) and i >= TURNS:
                        return
                    t = NT * l + UG * i + j
                    act.wait_ge(e_t, t + 1)
                    wait(act, e_seg, t - 2)
                    nc.scalar.copy(pairT[j % 3][:, 1:], psum[j % 2][:, 1:2 * P]).then_inc(e_ct, 1)

                def e_body(i, l=l):
                    for j in range(UG):
                        turned(i, j + 2)
                        t = NT * l + UG * i + j
                        act.wait_ge(e_msg, t + 1)
                        if isinstance(i, int) and i == 0 and j == 0:
                            held = zeros[:, 0:D]
                        else:
                            act.wait_ge(e_seg, t)
                            b = (j - 1) % UG
                            held = psum[4 + b // G][0:1, (b % G) * D:(b % G + 1) * D]
                        nc.scalar.copy(msg[j % 2][0:1, :], held).then_inc(e_carry, 1)
                turned(0, 0)
                turned(0, 1)
                turns(act, e_body, TURNS)
                phase_end(act, 4 + l)

        @block.vector
        def _(dve):
            order = Order(dve, s_order)
            nc.vector.memset(zeros[:, :], 0.0)
            nc.vector.memset(eps[:, :], EPS).then_inc(s_setup, 1)
            dve.wait_ge(s_const, 16 * CONSTS)
            for k in range(2):
                last = nc.vector.tensor_scalar(att_mat[:, k * HEADS:(k + 1) * HEADS], headmask[:, :], att_cols[:, k:k + 1],
                                               None, ALU.mult)
            last.then_inc(s_setup, 1)
            order.mark(nc.vector.tensor_tensor(repeat_f[:, :], dst_i[:, :], next_i[:, :], ALU.is_equal))
            nc.vector.memset(logit[:, :], 0.0)
            for k in range(3):
                nc.vector.memset(pairT[k][:, 0:1], 0.0)
            order.wait()
            nc.vector.scalar_tensor_tensor(out=last_idx[:, :], in0=repeat_f[:, :], scalar=float(SKIP), in1=dst_i[:, :],
                                           op0=ALU.mult, op1=ALU.add).then_inc(s_idx, 1)
            nc.vector.tensor_copy(dst_f[:, :], dst_i[:, :])
            nc.vector.tensor_copy(ends_f[:, :, 0], scan_i[:, :, P - 1])
            nc.vector.tensor_copy(ends_f[:, :, 1], scan_i[:, :, 1])
            for r in range(REL):
                last = nc.vector.tensor_single_scalar(is_r[:, r, :], etype_i[:, :], float(r), ALU.is_equal)
            order.mark(last)
            order.wait()
            for r in range(REL):
                for l in range(LAYERS):
                    for b in range(BASES):
                        c = comb_bc[:, l, r, b:b + 1]
                        if r == 0:
                            last = nc.vector.tensor_scalar(coef[:, l, :, b], is_r[:, r, :], c, None, ALU.mult)
                        else:
                            last = nc.vector.scalar_tensor_tensor(out=coef[:, l, :, b], in0=is_r[:, r, :], scalar=c,
                                                                  in1=coef[:, l, :, b], op0=ALU.mult, op1=ALU.add)
                order.mark(last)
                order.wait()
            dve.wait_ge(s_wt, 1)
            nc.vector.tensor_copy(w0[:, :], psum[0][:, 0:W0]).then_inc(s_w0, 1)

            def bn(rows, n):
                for j in range(n):
                    last = nc.vector.bn_stats(stats[:, j, :], rows[:, j, :])
                order.mark(last)

            def body_of(u1, v1, i1, u2, v2, i2):
                def add(l):
                    dve.wait_ge(n_r[l], u2 + 1)
                    nc.vector.tensor_tensor(hT[l + 1][:, :], rT[l][:, :], hT[l][:, :], ALU.add).then_inc(n_a[l], 1)
                if u1 is not None:
                    dve.wait_ge(n_x[v1], 16 * (i1 + 1))
                    bn(xn[v1], J)
                    ln_small(dve, order, J, None, None, n_var1, None)
                    ln_scale(dve, order, J, n_std1, u1 + 1, n_rs1)
                if u2 is not None:
                    add(0)
                if u1 is not None:
                    dve.wait_ge(n_m, u1 + 1)
                    ins = nc.vector.scalar_tensor_tensor(out=x1n[v1][:, :, :].rearrange("p j f -> p (j f)"), in0=psum[3][:, :], scalar=2.0,
                                                         in1=xn[v1][:, :, :].rearrange("p j f -> p (j f)"), op0=ALU.mult, op1=ALU.add)
                    ins.then_inc(n_x1, 1)
                    dve.wait_ge(n_x1, u1 + 1)
                    bn(x1n[v1], J)
                    ln_small(dve, order, J, None, None, n_var2, None)
                    if u2 is not None:
                        add(1)
                    ln_scale(dve, order, J, n_std2, u1 + 1, n_rs2)
                elif u2 is not None:
                    add(1)
                if u2 is not None:
                    add(2)
                    dve.wait_ge(n_tb[2], u2 + 1)
                    wait(dve, n_st[3][v2], 16 * i2)
                    nc.vector.tensor_tensor(on[v2][:, :, :].rearrange("p j f -> p (j f)"), psum[7][:, :],
                                            x1n[v2][:, :, :].rearrange("p j f -> p (j f)"), ALU.add).then_inc(n_out, 1)
            node_stream(dve, body_of, order)
            phase_end(dve, 1)

            def a_body(i):
                for u in range(2):
                    g = 2 * i + u
                    dve.wait_ge(a_x[u], 16 * 2 * G * (i + 1))
                    bn(xg[u][:, :, :, :].rearrange("p k j f -> p (k j) f"), 2 * G)
                    ln_small(dve, order, 2 * G, None, None, a_var, None)
                    dve.wait_ge(a_col[u], 16 * (i + 1))
                    wait(dve, a_st[u], 64 * i)
                    for j in range(G):
                        last = nc.vector.tensor_scalar(same[u][:, j, :], col_i[u][:, j, :], dst_f[:, bass.ds(g * G + j, 1)],
                                                       None, ALU.is_equal)
                    last.then_inc(a_same, 1)
                    ln_scale(dve, order, 2 * G, a_std, g + 1, a_rs)
                    dve.wait_ge(a_e0, g + 1)
                    at = bass.ds(g * (G * HEADS), G * HEADS)
                    a_src, a_own, a_dst = e0[u][:, 0, :, D:D + HEADS], e0[u][:, 1, :, D:D + HEADS], e0[u][:, 1, :, D + HEADS:W0]
                    nc.vector.tensor_tensor(logit[:, at].rearrange("p (g h) -> p g h", h=HEADS), a_src, a_dst, ALU.add)
                    nc.vector.tensor_tensor(own[:, at].rearrange("p (g h) -> p g h", h=HEADS), a_own, a_dst, ALU.add).then_inc(a_al, 1)
            turns(dve, a_body, TURNS, order)
            phase_end(dve, 2)

            n_log = NT * HEADS
            order.mark(nc.vector.scalar_tensor_tensor(out=logit[:, 0:n_log], in0=logit[:, 0:n_log], scalar=SLOPE,
                                                      in1=logit[:, 0:n_log], op0=ALU.mult, op1=ALU.max))
            order.mark(nc.vector.scalar_tensor_tensor(out=own[:, :], in0=own[:, :], scalar=SLOPE, in1=own[:, :],
                                                      op0=ALU.mult, op1=ALU.max))
            order.wait()
            nc.vector.memset(logit[0:1, :], -BIG).then_inc(m_t, 1)
            dve.wait_ge(m_pe, 1)
            flat = best[:, :, :].rearrange("p b c -> p (b c)")
            nc.vector.tensor_copy(flat[:, 0:512], psum[0][:, :])
            order.mark(nc.vector.tensor_copy(flat[:, 512:BLOCKS * P], psum[1][:, 0:BLOCKS * P - 512]))
            d = 1
            while d < P:
                order.wait()
                order.mark(nc.vector.tensor_tensor(differ[:, :, 0:P - d], scan_i[:, :, 0:P - d], scan_i[:, :, d:P], ALU.not_equal))
                order.wait()
                nc.vector.scalar_tensor_tensor(out=up[:, :, 0:P - d], in0=differ[:, :, 0:P - d], scalar=-BIG,
                                               in1=best[:, :, d:P], op0=ALU.mult, op1=ALU.add)
                order.mark(nc.vector.scalar_tensor_tensor(out=down[:, :, 0:P - d], in0=differ[:, :, 0:P - d], scalar=-BIG,
                                                          in1=best[:, :, 0:P - d], op0=ALU.mult, op1=ALU.add))
                order.wait()
                order.mark(nc.vector.tensor_tensor(best[:, :, 0:P - d], best[:, :, 0:P - d], up[:, :, 0:P - d], ALU.max))
                order.wait()
                order.mark(nc.vector.tensor_tensor(best[:, :, d:P], best[:, :, d:P], down[:, :, 0:P - d], ALU.max))
                d *= 2
            order.wait()
            for k, c in enumerate((P - 1, 1)):
                last = nc.vector.tensor_tensor(edge_max[:, k, :, :], tilesel[:, :].unsqueeze(1).broadcast_to([P, BLOCKS, 32]),
                                               best[:, :, c:c + 1].broadcast_to([P, BLOCKS, 32]), ALU.mult)
            last.then_inc(m_t, 1)
            dve.wait_ge(m_pe, 2)
            for k in range(2):
                order.wait()
                for b in range(BLOCKS):
                    last = nc.vector.tensor_scalar(pick[:, b, :], ends_i[:, k, :], ends_f[:, b, 1 - k:2 - k], -BIG,
                                                   ALU.not_equal, ALU.mult)
                order.mark(last)
                order.wait()
                order.mark(nc.vector.tensor_tensor(pick[:, :, :], pick[:, :, :],
                                                   psum[2 + k][:, 0:BLOCKS * 32].unsqueeze(1).broadcast_to([P, BLOCKS, BLOCKS * 32]), ALU.add))
                order.wait()
                order.mark(nc.vector.tensor_reduce(beyond[:, k, :], pick[:, :, :], AX.X, ALU.max))
                order.mark(nc.vector.tensor_tensor(differ[:, :, :], scan_i[:, :, :],
                                                   ends_f[:, :, 1 - k:2 - k].broadcast_to([P, BLOCKS, P]), ALU.not_equal))
                order.wait()
                order.mark(nc.vector.scalar_tensor_tensor(out=up[:, :, :], in0=differ[:, :, :], scalar=-BIG,
                                                          in1=beyond[:, k, :].unsqueeze(2).broadcast_to([P, BLOCKS, P]),
                                                          op0=ALU.mult, op1=ALU.add))
                order.wait()
                ins = nc.vector.tensor_tensor(best[:, :, :], best[:, :, :], up[:, :, :], ALU.max)
                order.mark(ins)
            order.wait()
            nc.vector.tensor_copy(down[:, :, :], best[:, :, :]).then_inc(m_t, 1)
            dve.wait_ge(m_pe, 3)
            nc.vector.tensor_tensor(top[:, 0:512], psum[0][:, :], own[:, 0:512], ALU.max)
            order.mark(nc.vector.tensor_tensor(top[:, 512:n_log], psum[1][:, 0:n_log - 512], own[:, 512:n_log], ALU.max))
            order.wait()
            nc.vector.tensor_tensor(logit[:, 0:n_log], logit[:, 0:n_log], top[:, :], ALU.subtract).then_inc(m_t, 2)
            nc.vector.tensor_tensor(own[:, :], own[:, :], top[:, :], ALU.subtract).then_inc(m_t, 2)
            dve.wait_ge(m_exp, 1)

            def weigh(g, u, i):
                w = logit[:, bass.ds(g * (G * HEADS), G * HEADS)].rearrange("p (g h) -> p g h", h=HEADS)
                dve.wait_ge(b_ld[u], 32 * (i + 1))
                wait(dve, b_seg, G * (g - 1))
                nc.vector.tensor_tensor(heads(msg0[u][:, :, 0:D]), heads(l0[u][:, :, 0:D]), per_head(w), ALU.mult)
                nc.vector.tensor_copy(msg0[u][:, :, 2 * D:SEG], w).then_inc(b_msg, 1)

            def b_body(i):
                for u in range(2):
                    g = 2 * i + u
                    at = bass.ds(g * (G * HEADS), G * HEADS)
                    w_own = own[:, at].rearrange("p (g h) -> p g h", h=HEADS)
                    if not (isinstance(g, int) and g + 1 >= 2 * TURNS):
                        weigh(g + 1, 1 - u, i + u)
                        dve.wait_ge(b_carry, G * (g + 1) + 1)
                    dve.wait_ge(b_seg, G * (g + 1))
                    sums = banks[:, G * u:G * (u + 1), :]
                    order.mark(nc.vector.tensor_tensor(den[:, :, :], sums[:, :, 2 * D:SEG], w_own, ALU.add))
                    order.wait()
                    order.mark(nc.vector.reciprocal(rden[:, :, :], den[:, :, :]))
                    order.wait()
                    order.mark(nc.vector.tensor_tensor(pself[:, :, :], w_own, rden[:, :, :], ALU.mult))
                    order.mark(nc.vector.tensor_tensor(heads(t_nbr[:, :, :]), heads(sums[:, :, 0:D]), per_head(rden[:, :, :]), ALU.mult))
                    order.wait()
                    order.mark(nc.vector.tensor_scalar_add(pself[:, :, :], pself[:, :, :], 1.0))
                    order.mark(nc.vector.tensor_tensor(t_nbr[:, :, :], t_nbr[:, :, :], sums[:, :, D:2 * D], ALU.add))
                    order.wait()
                    order.mark(nc.vector.tensor_tensor(heads(t_own[:, :, :]), heads(l0[u][:, :, D:2 * D]), per_head(pself[:, :, :]), ALU.mult))
                    order.wait()
                    order.mark(nc.vector.tensor_tensor(t_own[:, :, :], t_own[:, :, :], l0[u][:, :, 2 * D:3 * D], ALU.add))
                    order.wait()
                    wait(dve, b_st[u], 32 * i)
                    nc.vector.tensor_tensor(x1e[u][:, :, :], t_own[:, :, :], t_nbr[:, :, :], ALU.add).then_inc(b_x1, 1)
                    dve.wait_ge(b_x1, g + 1)
                    bn(x1e[u], G)
                    ln_small(dve, order, G, None, None, b_var, None)
                    ln_scale(dve, order, G, b_std, g + 1, b_rs)
            weigh(0, 0, 0)
            turns(dve, b_body, TURNS, order)
            phase_end(dve, 3)

            for l in range(LAYERS):
                def message(i, j, l=l):
                    i, j = i + j // UG, j % UG
                    if isinstance(i, int) and i >= TURNS:
                        return
                    t = NT * l + UG * i + j
                    y, m = psum[2 + j % 2], msg[j % 2]
                    dve.wait_ge(e_y, t + 1)
                    wait(dve, e_seg, t - 1)
                    for b in range(BASES):
                        c = coef[:, l, bass.ds(UG * i + j, 1), b]
                        if b == 0:
                            order.mark(nc.vector.tensor_scalar(m[:, :], y[:, 0:D], c, None, ALU.mult))
                        else:
                            order.wait()
                            ins = nc.vector.scalar_tensor_tensor(out=m[:, :], in0=y[:, b * D:(b + 1) * D], scalar=c, in1=m[:, :],
                                                                 op0=ALU.mult, op1=ALU.add)
                            if b < BASES - 1:
                                order.mark(ins)
                            else:
                                ins.then_inc(e_msg, 1)

                def e_body(i, l=l):
                    for j in range(UG):
                        message(i, j + 1)
                        if j % G == G - 1:
                            u = j // G
                            g = 2 * i + u
                            dve.wait_ge(e_seg, NT * l + G * (g + 1))
                            if not (isinstance(g, int) and g + 1 >= 2 * TURNS):
                                dve.wait_ge(e_carry, NT * l + G * (g + 1) + 1)
                            dve.wait_ge(e_ld[u], 32 * (TURNS * l + i + 1))
                            order.mark(nc.vector.tensor_tensor(
                                zsum[:, :, :], psum[4 + u][:, 0:G * D].rearrange("p (g f) -> p g f", g=G),
                                bias_row[:, l:l + 1, :].broadcast_to([P, G, D]), ALU.add))
                            order.wait()
                            if l < LAYERS - 1:
                                wait(dve, e_st[u], 16 * (TURNS * l + i))
                                to = hnew[u][:, :, :]
                            else:
                                to = zsum[:, :, :]
                            ins = nc.vector.scalar_tensor_tensor(
                                out=to.rearrange("p g f -> p (g f)"), in0=zsum[:, :, :].rearrange("p g f -> p (g f)"), scalar=0.0,
                                in1=hdst[u][:, :, :].rearrange("p g f -> p (g f)"), op0=ALU.max, op1=ALU.add)
                            if l == LAYERS - 1:
                                order.mark(ins)
                                order.wait()
                                dve.wait_ge(e_x1[u], 16 * (i + 1))
                                wait(dve, e_sc[u], 16 * G * i)
                                ins = nc.vector.tensor_tensor(hnew[u][:, :, :], zsum[:, :, :], x1e[u][:, :, :], ALU.add)
                            ins.then_inc(e_out, 1)
                message(0, 0)
                turns(dve, e_body, TURNS, order)
                phase_end(dve, 4 + l)

        @block.tensor
        def _(pe):
            pe.wait_ge(s_const, 16 * CONSTS)
            pe.wait_ge(s_setup, 2)
            nc.tensor.transpose(psum[0][:, 0:D], w_rows[:, :], ident[:, :])
            nc.tensor.matmul(psum[0][:, D:W0], w_rows[:, :], att_mat[:, :], start=True, stop=True).then_inc(s_wt, 1)
            pe.wait_ge(s_w0, 1)

            def turn(bank, blocks, n):
                for j in range(n):
                    last = nc.tensor.transpose(psum[bank][:, j * P:(j + 1) * P], blocks(j), ident[:, :])
                return last

            def body_of(u1, v1, i1, u2, v2, i2):
                def through(l, bank):
                    nc.tensor.matmul(psum[bank][:, :], wl[:, l, :], hT[l][:, :], start=True, stop=True).then_inc(n_z[l], 1)

                def back(l, bank):
                    turn(bank, lambda j: hT[l + 1][:, j * P:(j + 1) * P], J).then_inc(n_tb[l], 1)
                if u2 is not None:
                    pe.wait_ge(n_h0, u2 + 1)
                    turn(0, lambda j: h0n[v2][:, j, :], J).then_inc(n_t0, 1)
                    pe.wait_ge(n_h0t, u2 + 1)
                    through(0, 2)
                if u1 is not None:
                    pe.wait_ge(n_h, u1 + 1)
                    turn(1, lambda j: hn[:, j, :], J).then_inc(n_t, 1)
                if u2 is not None:
                    pe.wait_ge(n_a[0], u2 + 1)
                    through(1, 5)
                    back(0, 4)
                if u1 is not None:
                    pe.wait_ge(n_ht, u1 + 1)
                    for j in range(J):
                        last = nc.tensor.matmul(psum[3][:, j * D:(j + 1) * D], hnT[:, j * P:(j + 1) * P], w0[:, 0:D],
                                                start=True, stop=True)
                    last.then_inc(n_m, 1)
                if u2 is not None:
                    pe.wait_ge(n_a[1], u2 + 1)
                    through(2, 2)
                    back(1, 6)
                    pe.wait_ge(n_a[2], u2 + 1)
                    back(2, 7)
            node_stream(pe, body_of)
            phase_end(pe, 1)

            def a_body(i):
                for u in range(2):
                    g = 2 * i + u
                    pe.wait_ge(a_h, g + 1)
                    for k in range(2):
                        last = turn(2 * u + k, lambda j: ah[u][:, k * G + j, :], G)
                    last.then_inc(a_t, 1)
                    pe.wait_ge(a_ht, g + 1)
                    wait(pe, a_e0, g - 1)
                    for k in range(2):
                        for j in range(G):
                            last = nc.tensor.matmul(psum[4 + 2 * u + k][:, j * W0:(j + 1) * W0], ahT[u][:, k * G + j, :], w0[:, :],
                                                    start=True, stop=True)
                    last.then_inc(a_m, 1)
            turns(pe, a_body, TURNS)
            phase_end(pe, 2)

            pe.wait_ge(m_t, 1)
            for b in range(BLOCKS):
                last = nc.tensor.transpose(psum[b // 4][:, (b % 4) * P:(b % 4 + 1) * P], logit[:, b * P:(b + 1) * P], ident[:, :])
            last.then_inc(m_pe, 1)
            pe.wait_ge(m_t, 2)
            for k in range(2):
                last = nc.tensor.matmul(psum[2 + k][:, 0:BLOCKS * 32], headsel[:, :], edge_max[:, k, :, :].rearrange("p b c -> p (b c)"),
                                        start=True, stop=True)
            last.then_inc(m_pe, 1)
            pe.wait_ge(m_t, 3)
            for b in range(BLOCKS):
                last = nc.tensor.transpose(psum[b // 4][:, (b % 4) * P:(b % 4 + 1) * P], down[:, b, :], ident[:, :])
            last.then_inc(m_pe, 1)

            def b_body(i):
                for u in range(2):
                    g = 2 * i + u
                    pe.wait_ge(b_ld[u], 32 * (i + 1))
                    wait(pe, b_x1, g - 1)
                    for j in range(G):
                        pe.wait_ge(b_carry, G * g + j + 1)
                        nc.tensor.matmul(psum[G * u + j][:, 0:SEG], same[u][:, j, :], msg0[u][:, j, :], start=True, stop=True)\
                            .then_inc(b_seg, 1)
            turns(pe, b_body, TURNS)
            phase_end(pe, 3)

            for l in range(LAYERS):
                def to_turn(i, j, l=l):
                    i, j = i + j // UG, j % UG
                    if isinstance(i, int) and i >= TURNS:
                        return
                    t, u = NT * l + UG * i + j, j // G
                    if j % G == 0:
                        pe.wait_ge(e_hs[u], 16 * G * (TURNS * l + i + 1))
                        pe.wait_ge(e_ld[u], 32 * (TURNS * l + i + 1))
                    wait(pe, e_ct, t - 1)
                    nc.tensor.transpose(psum[j % 2][:, 0:P], hdst[u][:, j % G, :], ident[:, :])
                    nc.tensor.transpose(psum[j % 2][:, P:2 * P], hsrc[u][:, j % G, :], ident[:, :]).then_inc(e_t, 1)

                def project(i, j, l=l):
                    i, j = i + j // UG, j % UG
                    if isinstance(i, int) and i >= TURNS:
                        return
                    t = NT * l + UG * i + j
                    pe.wait_ge(e_ct, t + 1)
                    wait(pe, e_msg, t - 1)
                    nc.tensor.matmul(psum[2 + j % 2][:, :], pairT[j % 3][:, P:2 * P], basis_sb[:, l, :], start=True, stop=True)\
                        .then_inc(e_y, 1)

                def e_body(i, l=l):
                    for j in range(UG):
                        to_turn(i, j + 2)
                        project(i, j + 1)
                        t, u = NT * l + UG * i + j, j // G
                        if j % G == 0:
                            wait(pe, e_out, 2 * TURNS * l + 2 * i + u - 1)
                        pe.wait_ge(e_carry, t + 1)
                        at = psum[4 + u][:, (j % G) * D:(j % G + 1) * D]
                        nc.tensor.matmul(at, same[u][:, j % G, :], msg[j % 2][:, :], start=True, stop=False)
                        nc.tensor.matmul(at, pairT[j % 3][:, 0:P], wl[:, l, :], start=False, stop=True).then_inc(e_seg, 1)
                to_turn(0, 0)
                to_turn(0, 1)
                project(0, 0)
                turns(pe, e_body, TURNS)
                phase_end(pe, 4 + l)


def kernel(**inputs):
    import concourse.bacc as bacc
    from concourse.bass_utils import run_bass_kernel_spmd as run

    a = {k: np.asarray(v) for k, v in inputs.items()}
    src, dst, etype = a["src"], a["dst"], a["edge_type_8"]

    def slots(edge_values, first_column, pad):
        rest = np.full(NT * TE - E, pad, np.int32)
        body = np.concatenate([edge_values.astype(np.int32), rest]).reshape(NT, TE)
        return np.concatenate([first_column.reshape(NT, 1).astype(np.int32), body], axis=1)

    zero = np.zeros(NT, np.int32)
    padded = np.concatenate([dst, np.full(NT * TE - E, NO_EDGE, np.int32)]).reshape(NT, TE)
    ends = padded[:, -1]
    before = np.concatenate([np.full(1, NO_SEGMENT, np.int32), ends[:-1]])
    follow = np.concatenate([dst[1:], np.full(1, NO_SEGMENT, np.int32)])
    dst_slots = slots(dst, before, NO_EDGE)
    all_tiles = np.concatenate([dst_slots, np.full((BLOCKS * 32 - NT, P), NO_EDGE, np.int32)])
    scan = np.repeat(all_tiles.reshape(BLOCKS, 32, 1, P), HEADS, axis=2).transpose(1, 2, 0, 3).reshape(P, BLOCKS * P)
    tile_ends = np.stack([all_tiles[:, P - 1], all_tiles[:, 1]])
    tl, hd = np.arange(P) // HEADS, np.arange(P) % HEADS
    consts = np.concatenate([
        np.eye(P), np.arange(P)[:, None] // HD == np.arange(HEADS)[None, :],
        hd[:, None] == hd[None, :], tl[:, None] == np.arange(32)[None, :]], axis=1).astype(np.float32)
    arrays = {
        "x": a["x"], "src": slots(src, zero, 0).T, "dst_cols": dst_slots.T, "col_dst": slots(dst, ends, NO_EDGE),
        "next_dst": slots(follow, before, NO_EDGE).T, "dst_gather": slots(dst, zero, 0).T,
        "etype": slots(etype, zero, 0).T, "scan_dst": scan, "tile_ends": tile_ends, "consts": consts,
        "W": a["L0_gnn_W"], "att": np.stack([a["L0_gnn_att_src"].reshape(D), a["L0_gnn_att_dst"].reshape(D)], axis=1),
        "basis": a["L1_gnn_basis"], "comb": a["L1_gnn_comb"], "w_loop": a["L1_gnn_w_loop"], "bias": a["L1_gnn_bias"],
    }
    arrays = {f"in_{k}": np.ascontiguousarray(v) for k, v in arrays.items()}
    nc = bacc.Bacc("TRN2", target_bir_lowering=False, num_devices=1)
    aps = [nc.dram_tensor(k, v.shape, mybir.dt.from_np(v.dtype), kind="ExternalInput").ap() for k, v in arrays.items()]
    aps.append(nc.dram_tensor("out", (N, D), mybir.dt.float32, kind="ExternalOutput").ap())
    program(nc, *aps)
    return run(nc, [arrays], core_ids=[0]).results[0]["out"]
```

```python
import numpy as np
import concourse.bass as bass
from concourse import mybir
from contextlib import ExitStack

N, D, E = 50000, 128, 25000
HEADS, HD = 4, 32
REL, BASES, LAYERS = 8, 4, 3
P = 128
TE = P - 1
G = 3
UG = 2 * G
LG = 4 * G
L_TURNS = -(-E // (TE * LG))
NT = L_TURNS * LG
TURNS = NT // UG
SLOTS_G = 4
SLOTS = NT * P
J = 4
UNIT = P * J
UNITS = -(-N // UNIT)
LAST_UNIT = N - UNIT
AHEAD = 3
TAIL = TURNS - (UNITS - AHEAD) // 3
BLOCKS = -(-NT // 32)
PLACE_COLS = -(-N // P)
NO_EDGE, NO_SEGMENT = N, N + 1
SKIP = 65536
BIG = 1.0e30
EPS = 1e-5
SLOPE = 0.2
W0 = D + 2 * HEADS
SEG = 2 * D + HEADS
CONSTS = 18
GROUPS = NT // G
assert 3 * TURNS >= UNITS and 0 < TAIL < TURNS and NT * TE >= E


class Order:

    def __init__(self, eng, sem):
        self.eng, self.sem, self.base, self.k = eng, sem, 0, 0

    def mark(self, ins):
        ins.then_inc(self.sem, 1)
        self.k += 1

    def wait(self):
        self.eng.wait_ge(self.sem, self.base + self.k)


def turns(eng, body, n, order=None, tail=1):
    start = 0
    if order:
        start, order.k, order.base = order.base + order.k, 0, order.base + order.k
    body(0)
    per = order.k if order else 0
    with eng.Fori(1, n - tail) as i:
        if order:
            order.base, order.k = start + i * per, 0
        body(i)
    if order:
        order.base, order.k = start + (n - tail) * per, 0
    for i in range(n - tail, n):
        body(i)


def wait(eng, sem, value):
    if not (isinstance(value, int) and value <= 0):
        eng.wait_ge(sem, value)


def program(nc, x, src, dst_cols, col_dst, next_dst, dst_gather, etype, scan_dst, tile_ends, consts, W, att,
            basis, comb, w_loop, bias, out):
    fp32, i32 = mybir.dt.float32, mybir.dt.int32
    ALU, ACT, AX = mybir.AluOpType, mybir.ActivationFunctionType, mybir.AxisListType

    with ExitStack() as ctx:
        def sb(name, shape, dt=fp32):
            return ctx.enter_context(nc.sbuf_tensor(name, shape, dt))

        def sem(name):
            return ctx.enter_context(nc.semaphore(name))

        def dram(name, shape, dt=fp32):
            return nc.dram_tensor(name, shape, dt, kind="Internal").ap()

        h_tab = [dram(f"h_tab{l}", (N + SLOTS, D)) for l in range(LAYERS)]
        ident = sb("ident", [P, P])
        headmask = sb("headmask", [P, HEADS])
        w_rows = sb("w_rows", [P, D])
        att_cols = sb("att_cols", [P, 2])
        att_mat = sb("att_mat", [P, 2 * HEADS])
        w0 = sb("w0", [P, W0])
        wl = sb("wl", [P, LAYERS, D])
        basis_sb = sb("basis_sb", [P, LAYERS, BASES * D])
        bias_row = sb("bias_row", [P, LAYERS, D])
        bias_col = sb("bias_col", [P, LAYERS])
        eps = sb("eps", [P, 1])
        zeros = sb("zeros", [1, SEG])

        banks = ctx.enter_context(nc.psum_tensor("banks", [P, 8, 512], fp32))
        psum = [banks[:, b, :] for b in range(8)]

        s_const = sem("s_const")
        s_order = sem("s_order")
        s_setup = sem("s_setup")
        s_wt = sem("s_wt")
        s_w0 = sem("s_w0")
        s_phase = sem("s_phase")

        xn, x1n, h0n, h1n, h2n, on = ([sb(f"{n_}{v}", [P, J, D]) for v in range(3)]
                                      for n_ in ("xn", "x1n", "h0n", "h1n", "h2n", "on"))
        hn = sb("hn", [P, J, D])
        hnT = sb("hnT", [P, UNIT])
        hT = [[sb(f"hT{l}{v}", [P, UNIT]) for v in range(3)] for l in (0, 1, 2)]
        hT.append([sb("hT3", [P, UNIT])] * 3)
        rT = [sb(f"rT{l}", [P, UNIT]) for l in range(LAYERS)]

        class Norm:

            def __init__(self, name, n):
                self.n = n
                self.stats = sb(name + "_stats", [P, n, 6])
                self.sums = sb(name + "_sums", [P, 5, n])
                self.std, self.rstd, self.shift = (sb(name + k, [P, n]) for k in ("_std", "_rstd", "_shift"))

        norm1, norm2, norm_e = Norm("norm1", J), Norm("norm2", J), Norm("norm_e", 2 * G)
        norm_b = [Norm(f"norm_b{u}", G) for u in range(2)]

        n_x = [sem(f"n_xload{v}") for v in range(3)]
        n_var1, n_std1, n_rs1 = sem("n_var1"), sem("n_std1"), sem("n_rs1")
        n_h = sem("n_h")
        n_t = sem("n_t")
        n_ht = sem("n_ht")
        n_m = sem("n_m")
        n_x1 = sem("n_x1")
        n_var2, n_std2, n_rs2 = sem("n_var2"), sem("n_std2"), sem("n_rs2")
        n_h0 = sem("n_h0")
        n_t0, n_h0t = sem("n_t0"), sem("n_h0t")
        n_z = [sem(f"n_z{l}") for l in range(LAYERS)]
        n_r = [sem(f"n_r{l}") for l in range(LAYERS)]
        n_a = [sem(f"n_a{l}") for l in range(LAYERS)]
        n_tb = [sem(f"n_tb{l}") for l in range(LAYERS)]
        n_rows = [sem(f"n_rows{l}") for l in range(2)]
        n_out = sem("n_out")
        n_st = [[sem(f"n_st{k}_{v}") for v in range(3)] for k in range(4)]

        place_tab = dram("place_tab", (PLACE_COLS * P, 1), i32)
        l0_tab = dram("l0_tab", (SLOTS, 3 * D))
        same_tab = dram("same_tab", (SLOTS, P))
        x1_tab = dram("x1_tab", (SLOTS, D))
        src_i, dstg_i, dst_i, next_i, etype_i = (sb(n_, [P, NT], i32) for n_ in
                                                 ("src_i", "dstg_i", "dst_i", "next_i", "etype_i"))
        dst_f = sb("dst_f", [P, NT])
        is_r = sb("is_r", [P, REL, NT])
        repeat_f = sb("repeat_f", [P, NT])
        last_idx = sb("last_idx", [P, NT], i32)
        slot_row = sb("slot_row", [P, NT], i32)
        src_row = sb("src_row", [P, NT], i32)
        place_init = sb("place_init", [P, PLACE_COLS], i32)
        comb_bc = sb("comb_bc", [P, LAYERS, REL, BASES])
        coef = sb("coef", [P, LAYERS, NT, BASES])
        pool_idx = [sb(f"pool_idx{u}", [P, 2 * G], i32) for u in range(SLOTS_G)]
        place_idx = [sb(f"place_idx{u}", [P, G], i32) for u in range(2)]
        pool_val = [sb(f"pool_val{u}", [P, G], i32) for u in range(SLOTS_G)]
        headsel = sb("headsel", [P, P])
        tilesel = sb("tilesel", [P, 32])
        logit = sb("logit", [P, BLOCKS * 32 * HEADS])
        own = sb("own", [P, NT * HEADS])
        top = sb("top", [P, NT * HEADS])
        scan_i = sb("scan_i", [P, BLOCKS, P], i32)
        ends_i = sb("ends_i", [P, 2, BLOCKS * 32], i32)
        ends_f = sb("ends_f", [P, BLOCKS, 2])
        best, differ, up, down = (sb(n_, [P, BLOCKS, P]) for n_ in ("best", "differ", "up", "down"))
        edge_max = sb("edge_max", [P, 2, BLOCKS, 32])
        pick = sb("pick", [P, BLOCKS, BLOCKS * 32])
        beyond = sb("beyond", [P, 2, BLOCKS])

        xg = [sb(f"xg{u}", [P, 2, G, D]) for u in range(2)]
        ah = [sb(f"ah{u}", [P, 2 * G, D]) for u in range(2)]
        ahT = [sb(f"ahT{u}", [P, 2 * G, P]) for u in range(2)]
        e0 = [sb(f"e0{u}", [P, 2, G, W0]) for u in range(2)]
        col_i = [sb(f"col_i{u}", [P, G, P], i32) for u in range(2)]
        same = [sb(f"same{u}", [P, G, P]) for u in range(SLOTS_G)]
        l0 = [sb(f"l0{u}", [P, G, 3 * D]) for u in range(2)]
        msg0 = [sb(f"msg0{u}", [P, G, SEG]) for u in range(2)]
        den, rden, pself = (sb(n_, [P, G, HEADS]) for n_ in ("den", "rden", "pself"))
        free = [b[:, 0:G, :] for bufs in (xn, x1n, h0n, h1n, h2n, on) for b in bufs]
        x1e, hdst, hnew, hsrc = (free[k * SLOTS_G:(k + 1) * SLOTS_G] for k in range(4))
        zsum, t_nbr = free[4 * SLOTS_G:]
        t_own, t_att, *t_sum = (b[:, 0:G * D].rearrange("p (g f) -> p g f", g=G) for b in (hnT, *hT[0]))
        pairT = [sb(f"pairT{k}", [P, 2 * P]) for k in range(UG)]
        msg = [sb(f"msg{k}", [P, D]) for k in range(UG)]

        s_pool = sem("s_pool")
        s_iota = sem("s_iota")
        s_tab = sem("s_tab")
        s_idx = sem("s_idx")
        p_copy = sem("p_copy")
        p_sc = [sem(f"p_sc{u}") for u in range(2)]
        p_ga = [sem(f"p_ga{u}") for u in range(2)]
        p_row = sem("p_row")
        a_x = [sem(f"a_x{u}") for u in range(2)]
        a_col = [sem(f"a_col{u}") for u in range(2)]
        a_var, a_std, a_rs, a_h, a_t, a_ht, a_m, a_e0, a_al, a_same = (sem("a_" + n_) for n_ in
            ("var", "std", "rs", "h", "t", "ht", "m", "e0", "al", "same"))
        a_st = [sem(f"a_st{u}") for u in range(2)]
        m_t, m_pe, m_exp = sem("m_t"), sem("m_pe"), sem("m_exp")
        b_ld = [sem(f"b_ld{u}") for u in range(2)]
        b_st = [sem(f"b_st{u}") for u in range(2)]
        (b_plus, b_den, b_rden, b_nbr, b_att, b_pself, b_own, b_bn, b_half, b_total, b_sq, b_rstd) = (sem("b_" + n_) for n_ in
            ("plus", "den", "rden", "nbr", "att", "pself", "own", "bn", "half", "total", "sq", "rstd"))
        b_plain, b_msg, b_carry, b_seg, b_x1, b_var, b_std, b_rs, b_h = (sem("b_" + n_) for n_ in
            ("plain", "msg", "carry", "seg", "x1", "var", "std", "rs", "h"))
        e_ld = [sem(f"e_ld{u}") for u in range(SLOTS_G)]
        e_x1 = [sem(f"e_x1{u}") for u in range(SLOTS_G)]
        e_hs = [sem(f"e_hs{u}") for u in range(SLOTS_G)]
        e_st = [sem(f"e_st{u}") for u in range(SLOTS_G)]
        e_sc = [sem(f"e_sc{u}") for u in range(SLOTS_G)]
        e_z, e_relu = sem("e_z"), sem("e_relu")
        e_msg1, e_msg2 = sem("e_msg1"), sem("e_msg2")
        e_t, e_ct, e_y, e_first, e_msg, e_carry, e_seg, e_out = (sem("e_" + n_) for n_ in
            ("t", "ct", "y", "first", "msg", "carry", "seg", "out"))

        block = ctx.enter_context(nc.Block())

        def slot_rows(table, g, first=0, lo=0, hi=None):
            t = table[bass.ds(first + g * (G * P), G * P), lo:hi] if hi else table[bass.ds(first + g * (G * P), G * P), :]
            return t.rearrange("(j p) f -> p j f", p=P)

        def heads(ap):
            return ap.rearrange("p g (h d) -> p g h d", h=HEADS)

        def per_head(ap):
            return ap.unsqueeze(3).broadcast_to([P, G, HEADS, HD])

        def unit_rows(table, u):
            first = u * UNIT if not (isinstance(u, int) and u == UNITS - 1) else LAST_UNIT
            return table[bass.ds(first, UNIT), :].rearrange("(p j) f -> p j f", j=J)

        def phase_end(eng, k):
            eng.drain().then_inc(s_phase, 1)
            eng.wait_ge(s_phase, 4 * k)

        def variance(order, norm, ready):
            st = norm.stats
            total, half, m2, sq, var = (norm.sums[:, c, :] for c in range(5))
            order.wait()
            order.mark(nc.vector.tensor_tensor(half, st[:, :, 1], st[:, :, 4], ALU.subtract))
            order.mark(nc.vector.tensor_tensor(total, st[:, :, 1], st[:, :, 4], ALU.add))
            order.mark(nc.vector.tensor_tensor(m2, st[:, :, 2], st[:, :, 5], ALU.add))
            order.wait()
            order.mark(nc.vector.tensor_tensor(sq, half, half, ALU.mult))
            order.wait()
            nc.vector.scalar_tensor_tensor(out=var, in0=sq, scalar=D / 4.0, in1=m2, op0=ALU.mult,
                                           op1=ALU.add).then_inc(ready, 1)

        def norm_scale(dve, order, norm, root_ready, count, ready):
            dve.wait_ge(root_ready, count)
            order.mark(nc.vector.reciprocal(norm.rstd[:, :], norm.std[:, :]))
            order.wait()
            nc.vector.scalar_tensor_tensor(out=norm.shift[:, :], in0=norm.sums[:, 0, :], scalar=-0.5, in1=norm.rstd[:, :],
                                           op0=ALU.mult, op1=ALU.mult).then_inc(ready, 1)

        def streams(eng, step, order=None):
            for v in range(3):
                step(v - 3, v, -1)

            def fused(i):
                groups = [(2 * i + u, u, i) for u in range(2)]
                step(3 * i, 0, i, front=groups[0])
                step(3 * i + 1, 1, i, front=groups[1], back=groups[0])
                step(3 * i + 2, 2, i, back=groups[1])
            turns(eng, fused, TURNS, order, tail=TAIL)

        def in_range(u):
            return not isinstance(u, int) or 0 <= u < UNITS

        def flat(rows):
            return rows[:, :, :].rearrange("p j f -> p (j f)")

        @block.sync
        def _(sp):
            c = P + HEADS
            for dst_, src_ in (
                               (headsel[:, :], consts[:, c:c + P]), (tilesel[:, :], consts[:, c + P:c + P + 32]),
                               (src_i[:, :], src), (dstg_i[:, :], dst_gather), (dst_i[:, :], dst_cols),
                               (next_i[:, :], next_dst), (etype_i[:, :], etype),
                               (comb_bc[:, :, :, :], comb.partition_broadcast(P)),
                               (scan_i[:, :, :], scan_dst.rearrange("p (b c) -> p b c", b=BLOCKS)),
                               (ends_i[:, :, :], tile_ends.partition_broadcast(P)),
                               (ident[:, :], consts[:, 0:P]), (headmask[:, :], consts[:, P:P + HEADS]),
                               (w_rows[:, :], W), (att_cols[:, :], att),
                               (wl[:, :, :], w_loop.rearrange("l i o -> i l o")),
                               (basis_sb[:, :, :].rearrange("p l (b o) -> p l b o", b=BASES), basis.rearrange("l b i o -> i l b o")),
                               (bias_row[:, :, :], bias.partition_broadcast(P)),
                               (bias_col[:, :], bias.rearrange("l o -> o l"))):
                with nc.allow_non_contiguous_dma(reason="a few small constants"):
                    sp.dma_start(dst_, src_).then_inc(s_const, 16)

            def load_x(u, v):
                if in_range(u):
                    wait(sp, n_x1, u - 2)
                    sp.dma_start(xn[v][:, :, :], unit_rows(x, u)).then_inc(n_x[v], 16)

            def store_unit(k, u, v, ready, rows, table):
                if in_range(u):
                    sp.wait_ge(ready, u + 1)
                    if isinstance(u, int) and u == UNITS - 1:
                        sp.wait_ge(n_st[k][(v - 1) % 3], 16 * ((u - 1) // 3 + 1))
                    sp.dma_start(unit_rows(table, u), rows[v][:, :, :]).then_inc(n_st[k][v], 16)

            def a_load(g, u):
                wait(sp, a_same, g - 1)
                sp.dma_start(col_i[u][:, :, :].rearrange("p j c -> p (j c)"),
                             col_dst.rearrange("t c -> (t c)")[bass.ds(g * (G * P), G * P)].partition_broadcast(P))\
                    .then_inc(a_col[u], 16)

            def a_store(g, u):
                sp.wait_ge(a_same, g + 1)
                sp.dma_start(slot_rows(same_tab, g), same[u][:, :, :]).then_inc(a_st[u], 16)
                sp.wait_ge(a_e0, g + 1)
                for k in range(2):
                    sp.dma_start(slot_rows(l0_tab, g, lo=k * D, hi=(k + 1) * D), e0[u][:, k, :, 0:D]).then_inc(a_st[u], 16)
                sp.dma_start(slot_rows(l0_tab, g, lo=2 * D, hi=3 * D), xg[u][:, 1, :, :]).then_inc(a_st[u], 16)

            def step(k, v, i):
                load_x(k + AHEAD + 1, (v + 1) % 3)
                store_unit(2, k, v, n_rows[1], h2n, h_tab[2])
                store_unit(0, k + 2, (v + 2) % 3, n_h0, h0n, h_tab[0])
                store_unit(3, k, v, n_out, on, out)
                store_unit(1, k + 1, (v + 1) % 3, n_rows[0], h1n, h_tab[1])

            def fused(i):
                for v in range(3):
                    if v < 2 and not (isinstance(i, int) and i == TURNS - 1 and v == 1):
                        a_load(2 * i + v + 1, 1 - v)
                    step(3 * i + v, v, i)
                    if v > 0:
                        a_store(2 * i + v - 1, v - 1)
            load_x(0, 0)
            for v in range(3):
                step(v - 3, v, -1)
            a_load(0, 0)
            turns(sp, fused, TURNS, tail=TAIL)
            for k in range(4):
                for v in range(3):
                    sp.wait_ge(n_st[k][v], 16 * ((UNITS - 1 - v) // 3 + 1))
            for u in range(2):
                sp.wait_ge(a_st[u], 64 * TURNS)
            phase_end(sp, 1)

            def b_load(g, u):
                wait(sp, b_x1, g - 1)
                sp.dma_start(l0[u][:, :, :], slot_rows(l0_tab, g)).then_inc(b_ld[u], 16)
                sp.dma_start(same[u][:, :, :], slot_rows(same_tab, g)).then_inc(b_ld[u], 16)

            def b_body(i):
                for u in range(2):
                    g = 2 * i + u
                    if not (isinstance(g, int) and g + 1 >= 2 * TURNS):
                        b_load(g + 1, 1 - u)
                    sp.wait_ge(b_x1, g + 1)
                    sp.dma_start(slot_rows(x1_tab, g), x1e[u][:, :, :]).then_inc(b_st[u], 16)
                    if not (isinstance(g, int) and g == 0):
                        h_store(g - 1, 1 - u)

            def h_store(g, u):
                sp.wait_ge(b_h, g + 1)
                sp.dma_start(slot_rows(h_tab[0], g, N), hnew[u][:, :, :]).then_inc(b_st[u], 16)
            b_load(0, 0)
            turns(sp, b_body, TURNS)
            h_store(GROUPS - 1, 1)
            for u in range(2):
                sp.wait_ge(b_st[u], 32 * TURNS)
            phase_end(sp, 2)

            for l in range(LAYERS):
                def e_load(g, u, l=l):
                    wait(sp, e_out, GROUPS * l + g + 1 - SLOTS_G)
                    sp.dma_start(hdst[u][:, :, :], slot_rows(h_tab[l], g, N)).then_inc(e_ld[u], 16)
                    sp.dma_start(same[u][:, :, :], slot_rows(same_tab, g)).then_inc(e_ld[u], 16)
                    if l == LAYERS - 1:
                        sp.dma_start(x1e[u][:, :, :], slot_rows(x1_tab, g)).then_inc(e_x1[u], 16)

                def e_body(i, l=l):
                    for u in range(SLOTS_G):
                        g = SLOTS_G * i + u
                        if not (isinstance(g, int) and g + SLOTS_G - 1 >= GROUPS):
                            e_load(g + SLOTS_G - 1, (u - 1) % SLOTS_G)
                        if l < LAYERS - 1:
                            sp.wait_ge(e_out, GROUPS * l + g + 1)
                            sp.dma_start(slot_rows(h_tab[l + 1], g, N), hnew[u][:, :, :]).then_inc(e_st[u], 16)
                for u in range(SLOTS_G - 1):
                    e_load(u, u)
                turns(sp, e_body, L_TURNS)
                if l < LAYERS - 1:
                    for u in range(SLOTS_G):
                        sp.wait_ge(e_st[u], 16 * L_TURNS * (l + 1))
                phase_end(sp, 3 + l)

        @block.gpsimd
        def _(pool):
            order = Order(pool, p_copy)

            def pool_wait(s, value):
                if isinstance(value, int) and value <= 0:
                    return
                pool.wait_ge(s, value)
                pool.sem_inc(s_pool, 1)

            def copies(u, g, *pairs):
                for to, table in pairs:
                    ins = nc.gpsimd.tensor_copy(to, table[:, bass.ds(g * G, G)])
                    order.mark(ins)
                pool_wait(p_copy, order.base + order.k)

            nc.gpsimd.iota(place_init[:, :], [[1, PLACE_COLS]], base=0, channel_multiplier=PLACE_COLS).then_inc(s_iota, 1)
            nc.gpsimd.iota(slot_row[:, :], [[P, NT]], base=N, channel_multiplier=1).then_inc(s_iota, 1)
            pool.wait_ge(s_iota, 2)
            pool.dma_start(place_tab.rearrange("(p c) o -> p (c o)", p=P), place_init[:, :]).then_inc(s_tab, 16)
            pool.wait_ge(s_tab, 16)
            pool.wait_ge(s_idx, 1)

            def scatter_place(i):
                for u in range(2):
                    pool_wait(p_sc[u], 16 * G * i)
                    copies(u, 2 * i + u, (place_idx[u][:, :], last_idx), (pool_val[u][:, :], slot_row))
                    for j in range(G):
                        nc.gpsimd.indirect_dma_start(
                            out=place_tab, out_offset=bass.IndirectOffsetOnAxis(ap=place_idx[u][:, j:j + 1], axis=0),
                            in_=pool_val[u][:, j:j + 1], in_offset=None, bounds_check=N - 1, oob_is_err=False).then_inc(p_sc[u], 16)
            def gather_x(i):
                for u in range(2):
                    g = 2 * i + u
                    pool_wait(a_st[u], 64 * i)
                    copies(u, g, (pool_idx[u][:, 0:G], src_i), (pool_idx[u][:, G:2 * G], dstg_i))
                    for k in range(2):
                        for j in range(G):
                            nc.gpsimd.indirect_dma_start(
                                out=xg[u][:, k, j, :], out_offset=None, in_=x,
                                in_offset=bass.IndirectOffsetOnAxis(ap=pool_idx[u][:, k * G + j:k * G + j + 1], axis=0))\
                                .then_inc(a_x[u], 16)
            def early(i):
                gather_x(i)
                scatter_place(i)
            turns(pool, early, TURNS, order)
            for u in range(2):
                pool.wait_ge(p_sc[u], 16 * G * TURNS)

            def gather_place(i):
                for u in range(2):
                    g = 2 * i + u
                    copies(u, g, (pool_idx[u][:, 0:G], src_i))
                    for j in range(G):
                        nc.gpsimd.indirect_dma_start(
                            out=pool_val[u][:, j:j + 1], out_offset=None, in_=place_tab,
                            in_offset=bass.IndirectOffsetOnAxis(ap=pool_idx[u][:, j:j + 1], axis=0)).then_inc(p_ga[u], 16)
                for u in range(2):
                    pool_wait(p_ga[u], 16 * G * (i + 1))
                    order.mark(nc.gpsimd.tensor_copy(src_row[:, bass.ds((2 * i + u) * G, G)], pool_val[u][:, :]))
            turns(pool, gather_place, TURNS, order)


            for l in range(LAYERS):
                pool.wait_ge(s_phase, 4 * (2 + l))

                def gather_h(g, u, l=l):
                    pool_wait(e_t, NT * l + G * (g + 1 - SLOTS_G))
                    copies(u, g, (pool_idx[u][:, 0:G], src_row))
                    for j in range(G):
                        nc.gpsimd.indirect_dma_start(
                            out=hsrc[u][:, j, :], out_offset=None, in_=h_tab[l],
                            in_offset=bass.IndirectOffsetOnAxis(ap=pool_idx[u][:, j:j + 1], axis=0)).then_inc(e_hs[u], 16)

                def layer_turn(i, l=l):
                    for u in range(SLOTS_G):
                        g = SLOTS_G * i + u
                        if not (isinstance(g, int) and g + SLOTS_G - 1 >= GROUPS):
                            gather_h(g + SLOTS_G - 1, (u - 1) % SLOTS_G)
                        if l == LAYERS - 1:
                            pool_wait(e_sc[u], 16 * G * i)
                            copies(u, g, (pool_val[u][:, :], last_idx))
                            pool_wait(e_out, GROUPS * l + g + 1)
                            for j in range(G):
                                nc.gpsimd.indirect_dma_start(
                                    out=out, out_offset=bass.IndirectOffsetOnAxis(ap=pool_val[u][:, j:j + 1], axis=0),
                                    in_=hnew[u][:, j, :], in_offset=None, bounds_check=N - 1, oob_is_err=False).then_inc(e_sc[u], 16)
                for u in range(SLOTS_G - 1):
                    gather_h(u, u)
                turns(pool, layer_turn, L_TURNS, order)
            for u in range(SLOTS_G):
                pool.wait_ge(e_sc[u], 16 * G * L_TURNS)

        @block.scalar
        def _(act):
            act.wait_ge(s_setup, 1)

            def relu_rows(out_rows, in_rows, norm):
                for j in range(norm.n):
                    last = nc.scalar.activation(out_rows[:, j, :], in_rows[:, j, :], ACT.Relu,
                                                bias=norm.shift[:, j:j + 1], scale=norm.rstd[:, j:j + 1])
                return last

            def root(norm, var_ready, count, ready):
                act.wait_ge(var_ready, count)
                nc.scalar.activation(norm.std[:, :], norm.sums[:, 4, :], ACT.Sqrt, bias=eps[:, :], scale=1.0 / D).then_inc(ready, 1)

            def relu_bias(u, l, bank):
                if in_range(u):
                    act.wait_ge(n_z[l], u + 1)
                    nc.scalar.activation(rT[l][:, :], psum[bank], ACT.Relu, bias=bias_col[:, l:l + 1]).then_inc(n_r[l], 1)

            def step(k, v, i, front=None, back=None):
                u1, u2, u3, u4 = k + 3, k + 2, k + 1, k
                v2, i2, v3, i3 = (v + 2) % 3, i + (v + 2) // 3, (v + 1) % 3, i + (v + 1) // 3
                relu_bias(u4, 2, 0)
                relu_bias(u3, 0, 1)
                if back:
                    g, u, _ = back
                    act.wait_ge(a_t, g + 1)
                    for c in range(2):
                        last = nc.scalar.copy(flat(ahT[u][:, c * G:(c + 1) * G, :]), psum[5 + c][:, 0:G * P])
                    last.then_inc(a_ht, 1)
                if in_range(u2):
                    root(norm2, n_var2, u2 + 1, n_std2)
                if in_range(u1):
                    root(norm1, n_var1, u1 + 1, n_std1)
                if front:
                    root(norm_e, a_var, front[0] + 1, a_std)
                if in_range(u2):
                    act.wait_ge(n_rs2, u2 + 1)
                    wait(act, n_st[0][v2], 16 * i2)
                    relu_rows(h0n[v2], x1n[v2], norm2).then_inc(n_h0, 1)
                relu_bias(u3, 1, 1)
                if back:
                    act.wait_ge(a_m, g + 1)
                    wait(act, a_st[u], 64 * back[2])
                    wait(act, a_al, g - 1)
                    for c in range(2):
                        last = nc.scalar.copy(flat(e0[u][:, c, :, :]), psum[5 + c][:, 0:G * W0])
                    last.then_inc(a_e0, 1)
                if in_range(u1):
                    act.wait_ge(n_rs1, u1 + 1)
                    relu_rows(hn, xn[v], norm1).then_inc(n_h, 1)
                if in_range(u2):
                    act.wait_ge(n_t0, u2 + 1)
                    nc.scalar.copy(hT[0][v2][:, :], psum[2]).then_inc(n_h0t, 1)
                if in_range(u3):
                    act.wait_ge(n_tb[0], u3 + 1)
                    wait(act, n_st[1][v3], 16 * i3)
                    nc.scalar.copy(flat(h1n[v3]), psum[3]).then_inc(n_rows[0], 1)
                if in_range(u1):
                    act.wait_ge(n_t, u1 + 1)
                    nc.scalar.copy(hnT[:, :], psum[4]).then_inc(n_ht, 1)
                if front:
                    g, u, _ = front
                    act.wait_ge(a_rs, g + 1)
                    wait(act, a_t, g - 1)
                    relu_rows(ah[u], xg[u][:, :, :, :].rearrange("p k j f -> p (k j) f"), norm_e).then_inc(a_h, 1)

            streams(act, step)
            phase_end(act, 1)

            act.wait_ge(m_t, 7)
            nc.scalar.activation(logit[:, 0:NT * HEADS], logit[:, 0:NT * HEADS], ACT.Exp)
            nc.scalar.activation(own[:, :], own[:, :], ACT.Exp).then_inc(m_exp, 1)

            def plain(g, u, i):
                act.wait_ge(b_ld[u], 32 * (i + 1))
                wait(act, b_seg, G * (g - 1))
                nc.scalar.copy(msg0[u][:, :, D:2 * D], l0[u][:, :, 0:D]).then_inc(b_plain, 1)
                act.wait_ge(b_msg, g + 1)
                act.wait_ge(b_plain, g + 1)

            def carry(g, u, j):
                if j == 0 and isinstance(g, int) and g == 0:
                    held = zeros[:, :]
                else:
                    act.wait_ge(b_seg, G * g + j)
                    held = psum[(G * u + j - 1) % UG][0:1, 0:SEG]
                nc.scalar.copy(msg0[u][0:1, j, :], held).then_inc(b_carry, 1)

            def norm_relu(g, u, i):
                act.wait_ge(b_rs, g + 1)
                wait(act, b_st[u], 32 * i)
                relu_rows(hnew[u], x1e[u], norm_b[u]).then_inc(b_h, 1)

            def b_body(i):
                for u in range(2):
                    g = 2 * i + u
                    for j in range(1, G):
                        carry(g, u, j)
                    if not (isinstance(g, int) and g + 1 >= GROUPS):
                        plain(g + 1, 1 - u, i + u)
                        carry(g + 1, 1 - u, 0)
                    if not (isinstance(g, int) and g == 0):
                        norm_relu(g - 1, 1 - u, i + u - 1)
                    root(norm_b[u], b_var, g + 1, b_std)
            plain(0, 0, 0)
            carry(0, 0, 0)
            turns(act, b_body, TURNS)
            norm_relu(GROUPS - 1, 1, TURNS - 1)
            phase_end(act, 2)

            for l in range(LAYERS):
                def turned(i, j, l=l):
                    i, j = i + j // LG, j % LG
                    if isinstance(i, int) and i >= L_TURNS:
                        return
                    t = NT * l + LG * i + j
                    act.wait_ge(e_t, t + 1)
                    wait(act, e_seg, t - UG + 1)
                    nc.scalar.copy(pairT[j % UG][:, 1:], psum[j % 2][:, 1:2 * P]).then_inc(e_ct, 1)

                def first_term(i, j, l=l):
                    i, j = i + j // LG, j % LG
                    if isinstance(i, int) and i >= L_TURNS:
                        return
                    t = NT * l + LG * i + j
                    act.wait_ge(e_y, t + 1)
                    wait(act, e_seg, t - UG + 1)
                    nc.scalar.activation(msg[j % UG][:, :], psum[2 + j % 3][:, 0:D], ACT.Copy,
                                         scale=coef[:, l, bass.ds(LG * i + j, 1), 0]).then_inc(e_first, 1)

                def e_body(i, l=l):
                    for j in range(LG):
                        turned(i, j + 3)
                        t = NT * l + LG * i + j
                        act.wait_ge(e_msg, t + 1)
                        if isinstance(i, int) and i == 0 and j == 0:
                            held = zeros[:, 0:D]
                        else:
                            act.wait_ge(e_seg, t)
                            b = (j - 1) % UG
                            held = psum[5 + b // G][0:1, (b % G) * D:(b % G + 1) * D]
                        nc.scalar.copy(msg[j % UG][0:1, :], held).then_inc(e_carry, 1)
                        first_term(i, j + 2)
                for j in range(3):
                    turned(0, j)
                for j in range(2):
                    first_term(0, j)
                turns(act, e_body, L_TURNS)
                phase_end(act, 3 + l)

        @block.vector
        def _(dve):
            order = Order(dve, s_order)
            nc.vector.memset(zeros[:, :], 0.0)
            nc.vector.memset(eps[:, :], EPS).then_inc(s_setup, 1)
            dve.wait_ge(s_const, 16 * CONSTS)
            for k in range(2):
                last = nc.vector.tensor_scalar(att_mat[:, k * HEADS:(k + 1) * HEADS], headmask[:, :], att_cols[:, k:k + 1],
                                               None, ALU.mult)
            last.then_inc(s_setup, 1)
            order.mark(nc.vector.tensor_tensor(repeat_f[:, :], dst_i[:, :], next_i[:, :], ALU.is_equal))
            nc.vector.memset(logit[:, :], 0.0)
            for k in range(UG):
                nc.vector.memset(pairT[k][:, 0:1], 0.0)
            order.wait()
            nc.vector.scalar_tensor_tensor(out=last_idx[:, :], in0=repeat_f[:, :], scalar=float(SKIP), in1=dst_i[:, :],
                                           op0=ALU.mult, op1=ALU.add).then_inc(s_idx, 1)
            nc.vector.tensor_copy(dst_f[:, :], dst_i[:, :])
            nc.vector.tensor_copy(ends_f[:, :, 0], scan_i[:, :, P - 1])
            nc.vector.tensor_copy(ends_f[:, :, 1], scan_i[:, :, 1])
            for r in range(REL):
                last = nc.vector.tensor_single_scalar(is_r[:, r, :], etype_i[:, :], float(r), ALU.is_equal)
            order.mark(last)
            order.wait()
            for r in range(REL):
                for l in range(LAYERS):
                    for b in range(BASES):
                        c = comb_bc[:, l, r, b:b + 1]
                        if r == 0:
                            last = nc.vector.tensor_scalar(coef[:, l, :, b], is_r[:, r, :], c, None, ALU.mult)
                        else:
                            last = nc.vector.scalar_tensor_tensor(out=coef[:, l, :, b], in0=is_r[:, r, :], scalar=c,
                                                                  in1=coef[:, l, :, b], op0=ALU.mult, op1=ALU.add)
                order.mark(last)
                order.wait()
            dve.wait_ge(s_wt, 1)
            nc.vector.tensor_copy(w0[:, :], psum[0][:, 0:W0]).then_inc(s_w0, 1)

            def bn(rows, norm):
                for j in range(norm.n):
                    last = nc.vector.bn_stats(norm.stats[:, j, :], rows[:, j, :])
                order.mark(last)

            def add(u, v, l):
                if in_range(u):
                    dve.wait_ge(n_r[l], u + 1)
                    nc.vector.tensor_tensor(hT[l + 1][v][:, :], rT[l][:, :], hT[l][v][:, :], ALU.add).then_inc(n_a[l], 1)

            def step(k, v, i, front=None, back=None):
                u1, u2, u3, u4 = k + 3, k + 2, k + 1, k
                v2, v3 = (v + 2) % 3, (v + 1) % 3
                if in_range(u2):
                    dve.wait_ge(n_x1, u2 + 1)
                    bn(x1n[v2], norm2)
                    variance(order, norm2, n_var2)
                if in_range(u1):
                    dve.wait_ge(n_x[v], 16 * (i + 2))
                    bn(xn[v], norm1)
                    variance(order, norm1, n_var1)
                add(u4, v, 2)
                add(u3, v3, 0)
                if in_range(u2):
                    norm_scale(dve, order, norm2, n_std2, u2 + 1, n_rs2)
                if front:
                    g, u, gi = front
                    dve.wait_ge(a_x[u], 16 * 2 * G * (gi + 1))
                    bn(xg[u][:, :, :, :].rearrange("p k j f -> p (k j) f"), norm_e)
                    variance(order, norm_e, a_var)
                if in_range(u4):
                    dve.wait_ge(n_tb[1], u4 + 1)
                    wait(dve, n_st[2][v], 16 * i)
                    nc.vector.tensor_copy(flat(h2n[v]), psum[2]).then_inc(n_rows[1], 1)
                if in_range(u1):
                    norm_scale(dve, order, norm1, n_std1, u1 + 1, n_rs1)
                if in_range(u4):
                    dve.wait_ge(n_tb[2], u4 + 1)
                    wait(dve, n_st[3][v], 16 * i)
                    nc.vector.tensor_tensor(flat(on[v]), psum[0], flat(x1n[v]), ALU.add).then_inc(n_out, 1)
                if front:
                    norm_scale(dve, order, norm_e, a_std, g + 1, a_rs)
                    dve.wait_ge(a_col[u], 16 * (gi + 1))
                    wait(dve, a_st[u], 64 * gi)
                    for j in range(G):
                        last = nc.vector.tensor_scalar(same[u][:, j, :], col_i[u][:, j, :], dst_f[:, bass.ds(g * G + j, 1)],
                                                       None, ALU.is_equal)
                    last.then_inc(a_same, 1)
                add(u3, v3, 1)
                if back:
                    g, u, _ = back
                    dve.wait_ge(a_e0, g + 1)
                    at = bass.ds(g * (G * HEADS), G * HEADS)
                    a_src, a_own, a_dst = e0[u][:, 0, :, D:D + HEADS], e0[u][:, 1, :, D:D + HEADS], e0[u][:, 1, :, D + HEADS:W0]
                    nc.vector.tensor_tensor(logit[:, at].rearrange("p (g h) -> p g h", h=HEADS), a_src, a_dst, ALU.add)
                    nc.vector.tensor_tensor(own[:, at].rearrange("p (g h) -> p g h", h=HEADS), a_own, a_dst, ALU.add).then_inc(a_al, 1)
                if in_range(u1):
                    dve.wait_ge(n_m, u1 + 1)
                    if in_range(u4):
                        dve.wait_ge(n_out, u4 + 1)
                    nc.vector.scalar_tensor_tensor(out=flat(x1n[v]), in0=psum[4], scalar=2.0, in1=flat(xn[v]),
                                                   op0=ALU.mult, op1=ALU.add).then_inc(n_x1, 1)

            streams(dve, step, order)
            phase_end(dve, 1)

            n_log = NT * HEADS
            order.mark(nc.vector.scalar_tensor_tensor(out=logit[:, 0:n_log], in0=logit[:, 0:n_log], scalar=SLOPE,
                                                      in1=logit[:, 0:n_log], op0=ALU.mult, op1=ALU.max))
            order.mark(nc.vector.scalar_tensor_tensor(out=own[:, :], in0=own[:, :], scalar=SLOPE, in1=own[:, :],
                                                      op0=ALU.mult, op1=ALU.max))
            order.wait()
            nc.vector.memset(logit[0:1, :], -BIG).then_inc(m_t, 1)
            dve.wait_ge(m_pe, 1)
            nc.vector.tensor_copy(flat(best)[:, 0:512], psum[0])
            order.mark(nc.vector.tensor_copy(flat(best)[:, 512:BLOCKS * P], psum[1][:, 0:BLOCKS * P - 512]))
            d = 1
            while d < P:
                order.wait()
                order.mark(nc.vector.tensor_tensor(differ[:, :, 0:P - d], scan_i[:, :, 0:P - d], scan_i[:, :, d:P], ALU.not_equal))
                order.wait()
                nc.vector.scalar_tensor_tensor(out=up[:, :, 0:P - d], in0=differ[:, :, 0:P - d], scalar=-BIG,
                                               in1=best[:, :, d:P], op0=ALU.mult, op1=ALU.add)
                order.mark(nc.vector.scalar_tensor_tensor(out=down[:, :, 0:P - d], in0=differ[:, :, 0:P - d], scalar=-BIG,
                                                          in1=best[:, :, 0:P - d], op0=ALU.mult, op1=ALU.add))
                order.wait()
                order.mark(nc.vector.tensor_tensor(best[:, :, 0:P - d], best[:, :, 0:P - d], up[:, :, 0:P - d], ALU.max))
                order.wait()
                order.mark(nc.vector.tensor_tensor(best[:, :, d:P], best[:, :, d:P], down[:, :, 0:P - d], ALU.max))
                d *= 2
            order.wait()
            for k, c in enumerate((P - 1, 1)):
                last = nc.vector.tensor_tensor(edge_max[:, k, :, :], tilesel[:, :].unsqueeze(1).broadcast_to([P, BLOCKS, 32]),
                                               best[:, :, c:c + 1].broadcast_to([P, BLOCKS, 32]), ALU.mult)
            last.then_inc(m_t, 1)
            dve.wait_ge(m_pe, 2)
            for k in range(2):
                order.wait()
                for b in range(BLOCKS):
                    last = nc.vector.tensor_scalar(pick[:, b, :], ends_i[:, k, :], ends_f[:, b, 1 - k:2 - k], -BIG,
                                                   ALU.not_equal, ALU.mult)
                order.mark(last)
                order.wait()
                order.mark(nc.vector.tensor_tensor(pick[:, :, :], pick[:, :, :],
                                                   psum[2 + k][:, 0:BLOCKS * 32].unsqueeze(1).broadcast_to([P, BLOCKS, BLOCKS * 32]), ALU.add))
                order.wait()
                order.mark(nc.vector.tensor_reduce(beyond[:, k, :], pick[:, :, :], AX.X, ALU.max))
                order.mark(nc.vector.tensor_tensor(differ[:, :, :], scan_i[:, :, :],
                                                   ends_f[:, :, 1 - k:2 - k].broadcast_to([P, BLOCKS, P]), ALU.not_equal))
                order.wait()
                order.mark(nc.vector.scalar_tensor_tensor(out=up[:, :, :], in0=differ[:, :, :], scalar=-BIG,
                                                          in1=beyond[:, k, :].unsqueeze(2).broadcast_to([P, BLOCKS, P]),
                                                          op0=ALU.mult, op1=ALU.add))
                order.wait()
                ins = nc.vector.tensor_tensor(best[:, :, :], best[:, :, :], up[:, :, :], ALU.max)
                order.mark(ins)
            order.wait()
            nc.vector.tensor_copy(down[:, :, :], best[:, :, :]).then_inc(m_t, 1)
            dve.wait_ge(m_pe, 3)
            nc.vector.tensor_tensor(top[:, 0:512], psum[0][:, :], own[:, 0:512], ALU.max)
            order.mark(nc.vector.tensor_tensor(top[:, 512:n_log], psum[1][:, 0:n_log - 512], own[:, 512:n_log], ALU.max))
            order.wait()
            nc.vector.tensor_tensor(logit[:, 0:n_log], logit[:, 0:n_log], top[:, :], ALU.subtract).then_inc(m_t, 2)
            nc.vector.tensor_tensor(own[:, :], own[:, :], top[:, :], ALU.subtract).then_inc(m_t, 2)
            dve.wait_ge(m_exp, 1)

            def weigh(g, u, i):
                w = logit[:, bass.ds(g * (G * HEADS), G * HEADS)].rearrange("p (g h) -> p g h", h=HEADS)
                dve.wait_ge(b_ld[u], 32 * (i + 1))
                wait(dve, b_seg, G * (g - 1))
                nc.vector.tensor_tensor(heads(msg0[u][:, :, 0:D]), heads(l0[u][:, :, 0:D]), per_head(w), ALU.mult)
                nc.vector.tensor_copy(msg0[u][:, :, 2 * D:SEG], w).then_inc(b_msg, 1)
                nc.vector.tensor_tensor(t_sum[u][:, :, :], l0[u][:, :, D:2 * D], l0[u][:, :, 2 * D:3 * D], ALU.add).then_inc(b_plus, 1)

            def b_body(i):
                for u in range(2):
                    g = 2 * i + u
                    w_own = own[:, bass.ds(g * (G * HEADS), G * HEADS)].rearrange("p (g h) -> p g h", h=HEADS)
                    if not (isinstance(g, int) and g + 1 >= GROUPS):
                        weigh(g + 1, 1 - u, i + u)
                        dve.wait_ge(b_carry, G * (g + 1) + 1)
                    dve.wait_ge(b_seg, G * (g + 1))
                    sums = banks[:, G * u:G * (u + 1), :]
                    ins = nc.vector.tensor_tensor(den[:, :, :], sums[:, :, 2 * D:SEG], w_own, ALU.add)
                    ins.then_inc(b_den, 1)
                    dve.wait_ge(b_plus, g + 1)
                    nc.vector.tensor_tensor(t_nbr[:, :, :], t_sum[u][:, :, :], sums[:, :, D:2 * D], ALU.add).then_inc(b_nbr, 1)
                    dve.wait_ge(b_den, g + 1)
                    nc.vector.reciprocal(rden[:, :, :], den[:, :, :]).then_inc(b_rden, 1)
                    if not (isinstance(g, int) and g == 0):
                        scale_first(g - 1, 1 - u)
                    dve.wait_ge(b_rden, g + 1)
                    nc.vector.tensor_tensor(pself[:, :, :], w_own, rden[:, :, :], ALU.mult).then_inc(b_pself, 1)
                    nc.vector.tensor_tensor(heads(t_att[:, :, :]), heads(sums[:, :, 0:D]), per_head(rden[:, :, :]), ALU.mult)\
                        .then_inc(b_att, 1)
                    dve.wait_ge(b_pself, g + 1)
                    nc.vector.tensor_tensor(heads(t_own[:, :, :]), heads(l0[u][:, :, D:2 * D]), per_head(pself[:, :, :]), ALU.mult)\
                        .then_inc(b_own, 1)
                    dve.wait_ge(b_att, g + 1)
                    nc.vector.tensor_tensor(t_nbr[:, :, :], t_nbr[:, :, :], t_att[:, :, :], ALU.add).then_inc(b_nbr, 1)
                    if not (isinstance(g, int) and g == 0):
                        scale_second(g - 1, 1 - u)
                    dve.wait_ge(b_nbr, 2 * g + 2)
                    wait(dve, b_st[u], 32 * i)
                    nc.vector.tensor_tensor(x1e[u][:, :, :], t_own[:, :, :], t_nbr[:, :, :], ALU.add).then_inc(b_x1, 1)
                    dve.wait_ge(b_x1, g + 1)
                    for j in range(G):
                        last = nc.vector.bn_stats(norm_b[u].stats[:, j, :], x1e[u][:, j, :])
                    last.then_inc(b_bn, 1)
                    st, (total, half, m2, sq, var) = norm_b[u].stats, (norm_b[u].sums[:, c, :] for c in range(5))
                    dve.wait_ge(b_bn, g + 1)
                    nc.vector.tensor_tensor(half, st[:, :, 1], st[:, :, 4], ALU.subtract).then_inc(b_half, 1)
                    nc.vector.tensor_tensor(total, st[:, :, 1], st[:, :, 4], ALU.add).then_inc(b_total, 1)
                    nc.vector.tensor_tensor(m2, st[:, :, 2], st[:, :, 5], ALU.add).then_inc(b_half, 1)
                    dve.wait_ge(b_half, 2 * g + 2)
                    nc.vector.tensor_tensor(sq, half, half, ALU.mult).then_inc(b_sq, 1)
                    dve.wait_ge(b_sq, g + 1)
                    nc.vector.scalar_tensor_tensor(out=var, in0=sq, scalar=D / 4.0, in1=m2, op0=ALU.mult, op1=ALU.add).then_inc(b_var, 1)

            def scale_first(g, u):
                dve.wait_ge(b_std, g + 1)
                nc.vector.reciprocal(norm_b[u].rstd[:, :], norm_b[u].std[:, :]).then_inc(b_rstd, 1)

            def scale_second(g, u):
                dve.wait_ge(b_rstd, g + 1)
                nc.vector.scalar_tensor_tensor(out=norm_b[u].shift[:, :], in0=norm_b[u].sums[:, 0, :], scalar=-0.5,
                                               in1=norm_b[u].rstd[:, :], op0=ALU.mult, op1=ALU.mult).then_inc(b_rs, 1)
            weigh(0, 0, 0)
            turns(dve, b_body, TURNS)
            scale_first(GROUPS - 1, 1)
            scale_second(GROUPS - 1, 1)
            phase_end(dve, 2)

            for l in range(LAYERS):
                def term(i, j, b, l=l):
                    i, j = i + j // LG, j % LG
                    if isinstance(i, int) and i >= L_TURNS:
                        return
                    t = NT * l + LG * i + j
                    if b == 1:
                        dve.wait_ge(e_first, t + 1)
                    else:
                        dve.wait_ge(e_msg1 if b == 2 else e_msg2, t + 1)
                    nc.vector.scalar_tensor_tensor(
                        out=msg[j % UG][:, :], in0=psum[2 + j % 3][:, b * D:(b + 1) * D], scalar=coef[:, l, bass.ds(LG * i + j, 1), b],
                        in1=msg[j % UG][:, :], op0=ALU.mult, op1=ALU.add).then_inc((e_msg1, e_msg2, e_msg)[b - 1], 1)

                def sum_bias(g, u, l=l):
                    dve.wait_ge(e_seg, NT * l + G * (g + 1))
                    wait(dve, e_out, GROUPS * l + g)
                    nc.vector.tensor_tensor(
                        zsum[:, :, :], psum[5 + u % 2][:, 0:G * D].rearrange("p (g f) -> p g f", g=G),
                        bias_row[:, l:l + 1, :].broadcast_to([P, G, D]), ALU.add).then_inc(e_z, 1)

                def relu_add(g, u, i, l=l):
                    dve.wait_ge(e_ld[u], 32 * (L_TURNS * l + i + 1))
                    if l < LAYERS - 1:
                        wait(dve, e_st[u], 16 * (L_TURNS * l + i))
                        to = hnew[u][:, :, :]
                    else:
                        to = zsum[:, :, :]
                    dve.wait_ge(e_z, GROUPS * l + g + 1)
                    ins = nc.vector.scalar_tensor_tensor(
                        out=to.rearrange("p g f -> p (g f)"), in0=zsum[:, :, :].rearrange("p g f -> p (g f)"), scalar=0.0,
                        in1=hdst[u][:, :, :].rearrange("p g f -> p (g f)"), op0=ALU.max, op1=ALU.add)
                    ins.then_inc(e_relu if l == LAYERS - 1 else e_out, 1)

                def add_x1(g, u, i, l=l):
                    if l == LAYERS - 1:
                        dve.wait_ge(e_x1[u], 16 * (i + 1))
                        wait(dve, e_sc[u], 16 * G * i)
                        dve.wait_ge(e_relu, g + 1)
                        nc.vector.tensor_tensor(hnew[u][:, :, :], zsum[:, :, :], x1e[u][:, :, :], ALU.add).then_inc(e_out, 1)

                def e_body(i, l=l):
                    for j in range(LG):
                        u = j // G
                        g = SLOTS_G * i + u
                        put = j % G == 1 and not (isinstance(g, int) and g == 0)
                        term(i, j + 1, 1)
                        term(i, j, 3)
                        if put:
                            dve.wait_ge(e_carry, NT * l + G * g + 1)
                            sum_bias(g - 1, (u - 1) % SLOTS_G)
                        term(i, j + 1, 2)
                        if put:
                            relu_add(g - 1, (u - 1) % SLOTS_G, i if u else i - 1)
                        if j % G == 2 and not (isinstance(g, int) and g == 0):
                            add_x1(g - 1, (u - 1) % SLOTS_G, i if u else i - 1)
                term(0, 0, 1)
                term(0, 0, 2)
                turns(dve, e_body, L_TURNS)
                sum_bias(GROUPS - 1, SLOTS_G - 1)
                relu_add(GROUPS - 1, SLOTS_G - 1, L_TURNS - 1)
                add_x1(GROUPS - 1, SLOTS_G - 1, L_TURNS - 1)
                phase_end(dve, 3 + l)

        @block.tensor
        def _(pe):
            pe.wait_ge(s_const, 16 * CONSTS)
            pe.wait_ge(s_setup, 2)
            nc.tensor.transpose(psum[0][:, 0:D], w_rows[:, :], ident[:, :])
            nc.tensor.matmul(psum[0][:, D:W0], w_rows[:, :], att_mat[:, :], start=True, stop=True).then_inc(s_wt, 1)
            pe.wait_ge(s_w0, 1)

            def turn(bank, blocks, n):
                for j in range(n):
                    last = nc.tensor.transpose(psum[bank][:, j * P:(j + 1) * P], blocks(j), ident[:, :])
                return last

            def step(k, v, i, front=None, back=None):
                u1, u2, u3, u4 = k + 3, k + 2, k + 1, k
                v2, v3 = (v + 2) % 3, (v + 1) % 3

                def through(u, v, l, bank):
                    nc.tensor.matmul(psum[bank], wl[:, l, :], hT[l][v][:, :], start=True, stop=True).then_inc(n_z[l], 1)

                def turned_back(u, v, l, bank):
                    turn(bank, lambda j: hT[l + 1][v][:, j * P:(j + 1) * P], J).then_inc(n_tb[l], 1)
                if in_range(u4):
                    pe.wait_ge(n_a[1], u4 + 1)
                    wait(pe, n_out, u4)
                    through(u4, v, 2, 0)
                if in_range(u3):
                    pe.wait_ge(n_h0t, u3 + 1)
                    wait(pe, n_r[1], u3)
                    through(u3, v3, 0, 1)
                if in_range(u4):
                    turned_back(u4, v, 1, 2)
                if back:
                    g, u, _ = back
                    pe.wait_ge(a_h, g + 1)
                    wait(pe, a_e0, g)
                    for c in range(2):
                        last = turn(5 + c, lambda j: ah[u][:, c * G + j, :], G)
                    last.then_inc(a_t, 1)
                if in_range(u4):
                    pe.wait_ge(n_a[2], u4 + 1)
                    turned_back(u4, v, 2, 0)
                if in_range(u3):
                    pe.wait_ge(n_a[0], u3 + 1)
                    through(u3, v3, 1, 1)
                    wait(pe, n_rows[0], u3)
                    turned_back(u3, v3, 0, 3)
                if back:
                    pe.wait_ge(a_ht, g + 1)
                    for c in range(2):
                        for j in range(G):
                            last = nc.tensor.matmul(psum[5 + c][:, j * W0:(j + 1) * W0], ahT[u][:, c * G + j, :], w0[:, :],
                                                    start=True, stop=True)
                    last.then_inc(a_m, 1)
                if in_range(u2):
                    pe.wait_ge(n_h0, u2 + 1)
                    if in_range(u4):
                        pe.wait_ge(n_rows[1], u4 + 1)
                    turn(2, lambda j: h0n[v2][:, j, :], J).then_inc(n_t0, 1)
                if in_range(u1):
                    pe.wait_ge(n_h, u1 + 1)
                    wait(pe, n_x1, u1)
                    turn(4, lambda j: hn[:, j, :], J).then_inc(n_t, 1)
                    pe.wait_ge(n_ht, u1 + 1)
                    for j in range(J):
                        last = nc.tensor.matmul(psum[4][:, j * D:(j + 1) * D], hnT[:, j * P:(j + 1) * P], w0[:, 0:D],
                                                start=True, stop=True)
                    last.then_inc(n_m, 1)

            streams(pe, step)
            phase_end(pe, 1)

            pe.wait_ge(m_t, 1)
            for b in range(BLOCKS):
                last = nc.tensor.transpose(psum[b // 4][:, (b % 4) * P:(b % 4 + 1) * P], logit[:, b * P:(b + 1) * P], ident[:, :])
            last.then_inc(m_pe, 1)
            pe.wait_ge(m_t, 2)
            for k in range(2):
                last = nc.tensor.matmul(psum[2 + k][:, 0:BLOCKS * 32], headsel[:, :], edge_max[:, k, :, :].rearrange("p b c -> p (b c)"),
                                        start=True, stop=True)
            last.then_inc(m_pe, 1)
            pe.wait_ge(m_t, 3)
            for b in range(BLOCKS):
                last = nc.tensor.transpose(psum[b // 4][:, (b % 4) * P:(b % 4 + 1) * P], down[:, b, :], ident[:, :])
            last.then_inc(m_pe, 1)

            def b_body(i):
                for u in range(2):
                    g = 2 * i + u
                    pe.wait_ge(b_ld[u], 32 * (i + 1))
                    wait(pe, b_x1, g - 1)
                    for j in range(G):
                        pe.wait_ge(b_carry, G * g + j + 1)
                        nc.tensor.matmul(psum[G * u + j][:, 0:SEG], same[u][:, j, :], msg0[u][:, j, :], start=True, stop=True)\
                            .then_inc(b_seg, 1)
            turns(pe, b_body, TURNS)
            phase_end(pe, 2)

            for l in range(LAYERS):
                def to_turn(i, j, l=l):
                    i, j = i + j // LG, j % LG
                    if isinstance(i, int) and i >= L_TURNS:
                        return
                    t, u = NT * l + LG * i + j, j // G
                    if j % G == 0:
                        pe.wait_ge(e_hs[u], 16 * G * (L_TURNS * l + i + 1))
                        pe.wait_ge(e_ld[u], 32 * (L_TURNS * l + i + 1))
                    wait(pe, e_ct, t - 1)
                    nc.tensor.transpose(psum[j % 2][:, 0:P], hdst[u][:, j % G, :], ident[:, :])
                    nc.tensor.transpose(psum[j % 2][:, P:2 * P], hsrc[u][:, j % G, :], ident[:, :]).then_inc(e_t, 1)

                def project(i, j, l=l):
                    i, j = i + j // LG, j % LG
                    if isinstance(i, int) and i >= L_TURNS:
                        return
                    t = NT * l + LG * i + j
                    pe.wait_ge(e_ct, t + 1)
                    wait(pe, e_msg, t - 2)
                    nc.tensor.matmul(psum[2 + j % 3][:, :], pairT[j % UG][:, P:2 * P], basis_sb[:, l, :], start=True, stop=True)\
                        .then_inc(e_y, 1)

                def e_body(i, l=l):
                    for j in range(LG):
                        to_turn(i, j + 3)
                        project(i, j + 2)
                        t, u = NT * l + LG * i + j, j // G
                        if j % G == 0:
                            wait(pe, e_out, GROUPS * l + SLOTS_G * i + u - 1)
                        at = psum[5 + u % 2][:, (j % G) * D:(j % G + 1) * D]
                        pe.wait_ge(e_carry, t + 1)
                        nc.tensor.matmul(at, pairT[j % UG][:, 0:P], wl[:, l, :], start=True, stop=False)
                        nc.tensor.matmul(at, same[u][:, j % G, :], msg[j % UG][:, :], start=False, stop=True).then_inc(e_seg, 1)
                for j in range(3):
                    to_turn(0, j)
                for j in range(2):
                    project(0, j)
                turns(pe, e_body, L_TURNS)
                phase_end(pe, 3 + l)


def kernel(**inputs):
    import concourse.bacc as bacc
    from concourse.bass_utils import run_bass_kernel_spmd as run

    a = {k: np.asarray(v) for k, v in inputs.items()}
    src, dst, etype = a["src"], a["dst"], a["edge_type_8"]

    def slots(edge_values, first_column, pad):
        rest = np.full(NT * TE - E, pad, np.int32)
        body = np.concatenate([edge_values.astype(np.int32), rest]).reshape(NT, TE)
        return np.concatenate([first_column.reshape(NT, 1).astype(np.int32), body], axis=1)

    zero = np.zeros(NT, np.int32)
    padded = np.concatenate([dst, np.full(NT * TE - E, NO_EDGE, np.int32)]).reshape(NT, TE)
    ends = padded[:, -1]
    before = np.concatenate([np.full(1, NO_SEGMENT, np.int32), ends[:-1]])
    follow = np.concatenate([dst[1:], np.full(1, NO_SEGMENT, np.int32)])
    dst_slots = slots(dst, before, NO_EDGE)
    all_tiles = np.concatenate([dst_slots, np.full((BLOCKS * 32 - NT, P), NO_EDGE, np.int32)])
    scan = np.repeat(all_tiles.reshape(BLOCKS, 32, 1, P), HEADS, axis=2).transpose(1, 2, 0, 3).reshape(P, BLOCKS * P)
    tile_ends = np.stack([all_tiles[:, P - 1], all_tiles[:, 1]])
    tl, hd = np.arange(P) // HEADS, np.arange(P) % HEADS
    consts = np.concatenate([
        np.eye(P), np.arange(P)[:, None] // HD == np.arange(HEADS)[None, :],
        hd[:, None] == hd[None, :], tl[:, None] == np.arange(32)[None, :]], axis=1).astype(np.float32)
    arrays = {
        "x": a["x"], "src": slots(src, zero, 0).T, "dst_cols": dst_slots.T, "col_dst": slots(dst, ends, NO_EDGE),
        "next_dst": slots(follow, before, NO_EDGE).T, "dst_gather": slots(dst, zero, 0).T,
        "etype": slots(etype, zero, 0).T, "scan_dst": scan, "tile_ends": tile_ends, "consts": consts,
        "W": a["L0_gnn_W"], "att": np.stack([a["L0_gnn_att_src"].reshape(D), a["L0_gnn_att_dst"].reshape(D)], axis=1),
        "basis": a["L1_gnn_basis"], "comb": a["L1_gnn_comb"], "w_loop": a["L1_gnn_w_loop"], "bias": a["L1_gnn_bias"],
    }
    arrays = {f"in_{k}": np.ascontiguousarray(v) for k, v in arrays.items()}
    nc = bacc.Bacc("TRN2", target_bir_lowering=False, num_devices=1)
    aps = [nc.dram_tensor(k, v.shape, mybir.dt.from_np(v.dtype), kind="ExternalInput").ap() for k, v in arrays.items()]
    aps.append(nc.dram_tensor("out", (N, D), mybir.dt.float32, kind="ExternalOutput").ap())
    program(nc, *aps)
    return run(nc, [arrays], core_ids=[0]).results[0]["out"]
```

```python
import numpy as np
import concourse.bass as bass
from concourse import mybir
from contextlib import ExitStack

N, D, E = 50000, 128, 25000
HEADS, HD = 4, 32
REL, BASES, LAYERS = 8, 4, 3
P = 128
TE = P - 1
G = 3
UG = 2 * G
LG = 4 * G
L_TURNS = -(-E // (TE * LG))
NT = L_TURNS * LG
TURNS = NT // UG
SLOTS_G = 4
SLOTS = NT * P
J = 4
UNIT = P * J
UNITS = -(-N // UNIT)
LAST_UNIT = N - UNIT
AHEAD = 4
LOAD_AHEAD = 6
TAIL = TURNS - (UNITS - 4 - LOAD_AHEAD) // 3 - 1
BLOCKS = -(-NT // 32)
PLACE_COLS = -(-N // P)
NO_EDGE, NO_SEGMENT = N, N + 1
SKIP = 65536
BIG = 1.0e30
EPS = 1e-5
SLOPE = 0.2
W0 = D + 2 * HEADS
SEG = 2 * D + HEADS
PLACES = (NT - TURNS) // (2 * L_TURNS)
CONSTS, LATER_CONSTS = 9, 9
GROUPS = NT // G
assert 3 * TURNS >= UNITS and TURNS + 2 * L_TURNS * PLACES == NT and 0 < TAIL < TURNS and NT * TE >= E


class Order:

    def __init__(self, eng, sem):
        self.eng, self.sem, self.base, self.k = eng, sem, 0, 0

    def mark(self, ins):
        ins.then_inc(self.sem, 1)
        self.k += 1

    def wait(self, but=0):
        self.eng.wait_ge(self.sem, self.base + self.k - but)


def turns(eng, body, n, order=None, head=1, tail=1):
    start = order.base + order.k if order else 0
    per = 0

    def turn_starts(i):
        if order:
            order.base, order.k = start + i * per, 0
    for i in range(head):
        turn_starts(i)
        body(i)
        per = order.k if order else 0
    with eng.Fori(head, n - tail) as i:
        turn_starts(i)
        body(i)
    turn_starts(n - tail)
    for i in range(n - tail, n):
        body(i)


def wait(eng, sem, value):
    if not (isinstance(value, int) and value <= 0):
        eng.wait_ge(sem, value)


def program(nc, x, src, dst_cols, col_dst, next_dst, dst_gather, etype, scan_dst, tile_ends, consts, W, att,
            basis, comb, w_loop, bias, out):
    fp32, i32 = mybir.dt.float32, mybir.dt.int32
    ALU, ACT, AX = mybir.AluOpType, mybir.ActivationFunctionType, mybir.AxisListType

    with ExitStack() as ctx:
        def sb(name, shape, dt=fp32):
            return ctx.enter_context(nc.sbuf_tensor(name, shape, dt))

        def sem(name):
            return ctx.enter_context(nc.semaphore(name))

        def dram(name, shape, dt=fp32):
            return nc.dram_tensor(name, shape, dt, kind="Internal").ap()

        h_tab = [dram(f"h_tab{l}", (N + SLOTS, D)) for l in range(LAYERS)]
        ident = sb("ident", [P, P])
        headmask = sb("headmask", [P, HEADS])
        w_rows = sb("w_rows", [P, D])
        att_cols = sb("att_cols", [P, 2])
        att_mat = sb("att_mat", [P, 2 * HEADS])
        w0 = sb("w0", [P, W0])
        wl = sb("wl", [P, LAYERS, D])
        basis_sb = sb("basis_sb", [P, LAYERS, BASES * D])
        bias_row = sb("bias_row", [P, LAYERS, D])
        bias_col = sb("bias_col", [P, LAYERS])
        eps = sb("eps", [P, 1])
        zeros = sb("zeros", [1, SEG])
        ones = sb("ones", [1, P])

        banks = ctx.enter_context(nc.psum_tensor("banks", [P, 8, 512], fp32))
        psum = [banks[:, b, :] for b in range(8)]

        s_const = sem("s_const")
        s_later = sem("s_later")
        s_coef = sem("s_coef")
        s_order = sem("s_order")
        s_setup = sem("s_setup")
        s_wt = sem("s_wt")
        s_w0 = sem("s_w0")
        s_phase = sem("s_phase")

        xn, x1n, h0n, h1n, h2n, on = ([sb(f"{n_}{v}", [P, J, D]) for v in range(3)]
                                      for n_ in ("xn", "x1n", "h0n", "h1n", "h2n", "on"))
        hn = sb("hn", [P, J, D])
        hnT = sb("hnT", [P, UNIT])
        hT = [[sb(f"hT{l}{v}", [P, UNIT]) for v in range(3)] for l in (0, 1, 2)]
        rT = [sb(f"rT{l}", [P, UNIT]) for l in range(LAYERS - 1)]

        class Norm:

            def __init__(self, name, n):
                self.n = n
                self.stats = sb(name + "_stats", [P, n, 6])
                self.sums = sb(name + "_sums", [P, 5, n])
                self.std, self.rstd, self.shift = (sb(name + k, [P, n]) for k in ("_std", "_rstd", "_shift"))

        norm1, norm2, norm_e = Norm("norm1", J), Norm("norm2", J), Norm("norm_e", 2 * G)
        norm_b = [Norm(f"norm_b{u}", G) for u in range(2)]

        n_x = [sem(f"n_xload{v}") for v in range(3)]
        n_var1, n_std1, n_rs1 = sem("n_var1"), sem("n_std1"), sem("n_rs1")
        n_h = sem("n_h")
        n_t = sem("n_t")
        n_ht = sem("n_ht")
        n_m = sem("n_m")
        n_x1 = sem("n_x1")
        n_var2, n_std2, n_rs2 = sem("n_var2"), sem("n_std2"), sem("n_rs2")
        n_h0 = sem("n_h0")
        n_t0, n_h0t = sem("n_t0"), sem("n_h0t")
        n_z = [sem(f"n_z{l}") for l in range(LAYERS)]
        n_r = [sem(f"n_r{l}") for l in range(2)]
        n_a = [sem(f"n_a{l}") for l in range(2)]
        n_tb = [sem(f"n_tb{l}") for l in range(2)]
        n_rows = [sem(f"n_rows{l}") for l in range(2)]
        n_sum = sem("n_sum")
        n_out = sem("n_out")
        n_st = [[sem(f"n_st{k}_{v}") for v in range(3)] for k in range(4)]

        place_tab = dram("place_tab", (PLACE_COLS * P, 1), i32)
        l0_tab = dram("l0_tab", (SLOTS, 3 * D))
        same_tab = dram("same_tab", (SLOTS, P))
        x1_tab = dram("x1_tab", (SLOTS, D))
        src_i, dstg_i, dst_i, next_i, etype_i = (sb(n_, [P, NT], i32) for n_ in
                                                 ("src_i", "dstg_i", "dst_i", "next_i", "etype_i"))
        dst_f = sb("dst_f", [P, NT])
        is_r = sb("is_r", [P, REL, NT])
        repeat_f = sb("repeat_f", [P, NT])
        last_idx = sb("last_idx", [P, NT], i32)
        slot_row = sb("slot_row", [P, NT], i32)
        src_row = sb("src_row", [P, NT], i32)
        place_init = sb("place_init", [P, PLACE_COLS], i32)
        comb_bc = sb("comb_bc", [P, LAYERS, REL, BASES])
        coef = sb("coef", [P, LAYERS, NT, BASES])
        pool_idx = [sb(f"pool_idx{u}", [P, 2 * G], i32) for u in range(SLOTS_G)]
        place_idx = [sb(f"place_idx{u}", [P, PLACES], i32) for u in range(2)]
        place_val = [sb(f"place_val{u}", [P, PLACES], i32) for u in range(2)]
        turn_idx, turn_val = (sb(n_, [P, 1], i32) for n_ in ("turn_idx", "turn_val"))
        pool_val = [sb(f"pool_val{u}", [P, G], i32) for u in range(SLOTS_G)]
        headsel = sb("headsel", [P, P])
        tilesel = sb("tilesel", [P, 32])
        logit = sb("logit", [P, BLOCKS * 32 * HEADS])
        own = sb("own", [P, NT * HEADS])
        top = sb("top", [P, NT * HEADS])
        scan_i = sb("scan_i", [P, BLOCKS, P], i32)
        ends_i = sb("ends_i", [P, 2, BLOCKS * 32], i32)
        ends_f = sb("ends_f", [P, BLOCKS, 2])
        best, differ, up, down = (sb(n_, [P, BLOCKS, P]) for n_ in ("best", "differ", "up", "down"))
        edge_max = sb("edge_max", [P, 2, BLOCKS, 32])
        pick = sb("pick", [P, BLOCKS, BLOCKS * 32])
        beyond = sb("beyond", [P, 2, BLOCKS])

        xg = [sb(f"xg{u}", [P, 2, G, D]) for u in range(2)]
        ah = [sb(f"ah{u}", [P, 2 * G, D]) for u in range(2)]
        ahT = [sb(f"ahT{u}", [P, 2 * G, P]) for u in range(2)]
        e0 = [sb(f"e0{u}", [P, 2, G, W0]) for u in range(2)]
        col_i = [sb(f"col_i{u}", [P, G, P], i32) for u in range(2)]
        same = [sb(f"same{u}", [P, G, P]) for u in range(SLOTS_G)]
        l0 = [sb(f"l0{u}", [P, G, 3 * D]) for u in range(SLOTS_G)]
        msg0 = [sb(f"msg0{u}", [P, G, SEG]) for u in range(2)]
        den, rden, pself = (sb(n_, [P, G, HEADS]) for n_ in ("den", "rden", "pself"))
        free = [b[:, 0:G, :] for bufs in (xn, x1n, h0n, h1n, h2n, on) for b in bufs]
        x1e, hdst, hnew, hsrc = (free[k * SLOTS_G:(k + 1) * SLOTS_G] for k in range(4))
        zsum, t_nbr = free[4 * SLOTS_G:]
        t_own, t_att, *t_sum = (b[:, 0:G * D].rearrange("p (g f) -> p g f", g=G) for b in (hnT, *hT[0]))
        pairT = [sb(f"pairT{k}", [P, 2 * P]) for k in range(UG)]
        msg = [sb(f"msg{k}", [P, D]) for k in range(UG)]

        s_pool = sem("s_pool")
        s_iota = sem("s_iota")
        s_tab = sem("s_tab")
        s_idx = sem("s_idx")
        p_copy = sem("p_copy")
        p_aidx = sem("p_aidx")
        p_turn, p_tidx = sem("p_turn"), sem("p_tidx")
        p_sc = [sem(f"p_sc{u}") for u in range(2)]
        p_ga = [sem(f"p_ga{u}") for u in range(SLOTS_G)]
        a_x = [sem(f"a_x{u}") for u in range(2)]
        a_col = [sem(f"a_col{u}") for u in range(2)]
        a_var, a_std, a_rs, a_h, a_t, a_ht, a_m, a_e0, a_al, a_same = (sem("a_" + n_) for n_ in
            ("var", "std", "rs", "h", "t", "ht", "m", "e0", "al", "same"))
        a_st = [sem(f"a_st{u}") for u in range(2)]
        m_t, m_pe, m_exp = sem("m_t"), sem("m_pe"), sem("m_exp")
        b_ld = [sem(f"b_ld{u}") for u in range(SLOTS_G)]
        b_st = [sem(f"b_st{u}") for u in range(SLOTS_G)]
        (b_plus, b_den, b_rden, b_nbr, b_att, b_pself, b_own, b_bn, b_half, b_sq, b_rstd) = (sem("b_" + n_) for n_ in
            ("plus", "den", "rden", "nbr", "att", "pself", "own", "bn", "half", "sq", "rstd"))
        b_plain, b_msg, b_carry, b_seg, b_x1, b_var, b_std, b_rs, b_h = (sem("b_" + n_) for n_ in
            ("plain", "msg", "carry", "seg", "x1", "var", "std", "rs", "h"))
        e_ld = [sem(f"e_ld{u}") for u in range(SLOTS_G)]
        e_x1 = [sem(f"e_x1{u}") for u in range(SLOTS_G)]
        e_hs = [sem(f"e_hs{u}") for u in range(SLOTS_G)]
        e_st = [sem(f"e_st{u}") for u in range(SLOTS_G)]
        e_sc = [sem(f"e_sc{u}") for u in range(SLOTS_G)]
        e_oidx = sem("e_oidx")
        e_z, e_relu = sem("e_z"), sem("e_relu")
        e_msg1, e_msg2 = sem("e_msg1"), sem("e_msg2")
        e_t, e_ct, e_y, e_first, e_msg, e_carry, e_seg, e_out = (sem("e_" + n_) for n_ in
            ("t", "ct", "y", "first", "msg", "carry", "seg", "out"))

        block = ctx.enter_context(nc.Block())

        def slot_rows(table, g, first=0, lo=0, hi=None):
            t = table[bass.ds(first + g * (G * P), G * P), lo:hi] if hi else table[bass.ds(first + g * (G * P), G * P), :]
            return t.rearrange("(j p) f -> p j f", p=P)

        def heads(ap):
            return ap.rearrange("p g (h d) -> p g h d", h=HEADS)

        def per_head(ap):
            return ap.unsqueeze(3).broadcast_to([P, G, HEADS, HD])

        def unit_rows(table, u):
            first = u * UNIT if not (isinstance(u, int) and u == UNITS - 1) else LAST_UNIT
            return table[bass.ds(first, UNIT), :].rearrange("(p j) f -> p j f", j=J)

        def phase_end(eng, k):
            eng.drain().then_inc(s_phase, 1)
            eng.wait_ge(s_phase, 4 * k)

        def variance(order, norm, ready):
            st = norm.stats
            total, half, m2, sq, var = (norm.sums[:, c, :] for c in range(5))
            order.wait()
            order.mark(nc.vector.tensor_tensor(half, st[:, :, 1], st[:, :, 4], ALU.subtract))
            order.mark(nc.vector.tensor_tensor(m2, st[:, :, 2], st[:, :, 5], ALU.add))
            order.wait(but=1)
            order.mark(nc.vector.tensor_tensor(sq, half, half, ALU.mult))
            nc.vector.tensor_tensor(total, st[:, :, 1], st[:, :, 4], ALU.add)
            order.wait()
            nc.vector.scalar_tensor_tensor(out=var, in0=sq, scalar=D / 4.0, in1=m2, op0=ALU.mult,
                                           op1=ALU.add).then_inc(ready, 1)

        def norm_scale(dve, order, norm, root_ready, count, ready):
            dve.wait_ge(root_ready, count)
            order.mark(nc.vector.reciprocal(norm.rstd[:, :], norm.std[:, :]))
            order.wait()
            nc.vector.scalar_tensor_tensor(out=norm.shift[:, :], in0=norm.sums[:, 0, :], scalar=-0.5, in1=norm.rstd[:, :],
                                           op0=ALU.mult, op1=ALU.mult).then_inc(ready, 1)

        def streams(eng, step, order=None):
            for k in range(-AHEAD, 0):
                step(k, k % 3, k // 3)

            def turn(i):
                for v in range(3):
                    step(3 * i + v, v, i)
            turns(eng, turn, TURNS, order, tail=TAIL)

        def places(k, v, i):
            def at(ahead):
                return k + ahead, (v + ahead) % 3, i + (v + ahead) // 3

            def group(first):
                u, turn = (v - first) % 3, i + (v - first) // 3
                return (None if u == 2 or isinstance(turn, int) and not 0 <= turn < TURNS else 2 * turn + u), u, turn
            return at, group

        def done(eng, sem_, count):
            wait(eng, sem_, min(count, UNITS) if isinstance(count, int) else count)

        def in_range(u):
            return not isinstance(u, int) or 0 <= u < UNITS

        def flat(rows):
            return rows[:, :, :].rearrange("p j f -> p (j f)")

        @block.sync
        def _(sp):
            c = P + HEADS

            def constants(done_, *pairs):
                for to, table in pairs:
                    with nc.allow_non_contiguous_dma(reason="a few small constants"):
                        sp.dma_start(to, table).then_inc(done_, 16)
            constants(s_const,
                      (src_i[:, :], src), (dstg_i[:, :], dst_gather), (ident[:, :], consts[:, 0:P]),
                      (w_rows[:, :], W), (headmask[:, :], consts[:, P:P + HEADS]), (att_cols[:, :], att),
                      (wl[:, :, :], w_loop.rearrange("l i o -> i l o")),
                      (bias_col[:, :], bias.rearrange("l o -> o l")), (bias_row[:, :, :], bias.partition_broadcast(P)))
            for u in range(LOAD_AHEAD - AHEAD):
                sp.dma_start(xn[u][:, :, :], unit_rows(x, u)).then_inc(n_x[u], 16)
            constants(s_later,
                      (dst_i[:, :], dst_cols), (next_i[:, :], next_dst), (etype_i[:, :], etype),
                      (headsel[:, :], consts[:, c:c + P]), (tilesel[:, :], consts[:, c + P:c + P + 32]),
                      (comb_bc[:, :, :, :], comb.partition_broadcast(P)),
                      (scan_i[:, :, :], scan_dst.rearrange("p (b c) -> p b c", b=BLOCKS)),
                      (ends_i[:, :, :], tile_ends.partition_broadcast(P)),
                      (basis_sb[:, :, :].rearrange("p l (b o) -> p l b o", b=BASES), basis.rearrange("l b i o -> i l b o")))

            def load_x(unit):
                u, v, _ = unit
                if in_range(u):
                    done(sp, n_x1, u - 2)
                    sp.dma_start(xn[v][:, :, :], unit_rows(x, u)).then_inc(n_x[v], 16)

            def store_unit(unit, k, ready, rows, table):
                u, v, _ = unit
                if in_range(u):
                    sp.wait_ge(ready, u + 1)
                    if isinstance(u, int) and u == UNITS - 1:
                        sp.wait_ge(n_st[k][(v - 1) % 3], 16 * ((u - 1) // 3 + 1))
                    sp.dma_start(unit_rows(table, u), rows[v][:, :, :]).then_inc(n_st[k][v], 16)

            def a_load(place):
                g, u, _ = place
                if g is not None:
                    wait(sp, a_same, g - 1)
                    sp.dma_start(col_i[u][:, :, :].rearrange("p j c -> p (j c)"),
                                 col_dst.rearrange("t c -> (t c)")[bass.ds(g * (G * P), G * P)].partition_broadcast(P))\
                        .then_inc(a_col[u], 16)

            def a_store(place):
                g, u, _ = place
                if g is not None:
                    sp.wait_ge(a_same, g + 1)
                    sp.dma_start(slot_rows(same_tab, g), same[u][:, :, :]).then_inc(a_st[u], 16)
                    sp.wait_ge(a_e0, g + 1)
                    for k in range(2):
                        sp.dma_start(slot_rows(l0_tab, g, lo=k * D, hi=(k + 1) * D), e0[u][:, k, :, 0:D]).then_inc(a_st[u], 16)
                    sp.dma_start(slot_rows(l0_tab, g, lo=2 * D, hi=3 * D), xg[u][:, 1, :, :]).then_inc(a_st[u], 16)

            def step(k, v, i):
                at, group = places(k, v, i)
                a_load(group(-1))
                load_x(at(LOAD_AHEAD))
                a_store(group(0))
                store_unit(at(1), 2, n_rows[1], h2n, h_tab[2])
                store_unit(at(0), 1, n_rows[0], h1n, h_tab[1])
                store_unit(at(1), 3, n_out, on, out)
                store_unit(at(2), 0, n_h0, h0n, h_tab[0])

            streams(sp, step)
            for k in range(4):
                for v in range(3):
                    sp.wait_ge(n_st[k][v], 16 * ((UNITS - 1 - v) // 3 + 1))
            for u in range(2):
                sp.wait_ge(a_st[u], 64 * TURNS)
            phase_end(sp, 1)

            def b_load(g, u):
                sp.dma_start(l0[u][:, :, :], slot_rows(l0_tab, g)).then_inc(b_ld[u], 16)
                sp.dma_start(same[u][:, :, :], slot_rows(same_tab, g)).then_inc(b_ld[u], 16)

            def h_store(g, u):
                sp.wait_ge(b_h, g + 1)
                sp.dma_start(slot_rows(h_tab[0], g, N), hnew[u][:, :, :]).then_inc(b_st[u], 16)

            def b_body(i):
                for u in range(SLOTS_G):
                    g = SLOTS_G * i + u
                    sp.wait_ge(b_x1, g + 1)
                    if not (isinstance(g, int) and g + SLOTS_G >= GROUPS):
                        b_load(g + SLOTS_G, u)
                    sp.dma_start(slot_rows(x1_tab, g), x1e[u][:, :, :]).then_inc(b_st[u], 16)
                    if not (isinstance(g, int) and g < 2):
                        h_store(g - 2, (u - 2) % SLOTS_G)
            for u in range(SLOTS_G):
                b_load(u, u)
            turns(sp, b_body, L_TURNS)
            for k in (2, 1):
                h_store(GROUPS - k, SLOTS_G - k)
            for u in range(SLOTS_G):
                sp.wait_ge(b_st[u], 32 * L_TURNS)
            phase_end(sp, 2)

            for l in range(LAYERS):
                def e_load(g, u, l=l):
                    wait(sp, e_out, GROUPS * l + g + 1 - SLOTS_G)
                    sp.dma_start(hdst[u][:, :, :], slot_rows(h_tab[l], g, N)).then_inc(e_ld[u], 16)
                    sp.dma_start(same[u][:, :, :], slot_rows(same_tab, g)).then_inc(e_ld[u], 16)
                    if l == LAYERS - 1:
                        sp.dma_start(x1e[u][:, :, :], slot_rows(x1_tab, g)).then_inc(e_x1[u], 16)

                def e_body(i, l=l):
                    for u in range(SLOTS_G):
                        g = SLOTS_G * i + u
                        if not (isinstance(g, int) and g + SLOTS_G - 1 >= GROUPS):
                            e_load(g + SLOTS_G - 1, (u - 1) % SLOTS_G)
                        if l < LAYERS - 1:
                            sp.wait_ge(e_out, GROUPS * l + g + 1)
                            sp.dma_start(slot_rows(h_tab[l + 1], g, N), hnew[u][:, :, :]).then_inc(e_st[u], 16)
                for u in range(SLOTS_G - 1):
                    e_load(u, u)
                turns(sp, e_body, L_TURNS)
                if l < LAYERS - 1:
                    for u in range(SLOTS_G):
                        sp.wait_ge(e_st[u], 16 * L_TURNS * (l + 1))
                phase_end(sp, 3 + l)

        @block.gpsimd
        def _(pool):
            order = Order(pool, p_copy)

            def pool_wait(s, value):
                if isinstance(value, int) and value <= 0:
                    return
                pool.wait_ge(s, value)
                pool.sem_inc(s_pool, 1)

            def copies(u, g, *pairs):
                for to, table in pairs:
                    ins = nc.gpsimd.tensor_copy(to, table[:, bass.ds(g * G, G)])
                    order.mark(ins)
                pool_wait(p_copy, order.base + order.k)

            pool.wait_ge(s_const, 16 * CONSTS)
            nc.gpsimd.iota(place_init[:, :], [[1, PLACE_COLS]], base=0, channel_multiplier=PLACE_COLS).then_inc(s_iota, 1)
            nc.gpsimd.iota(slot_row[:, :], [[P, NT]], base=N, channel_multiplier=1).then_inc(s_iota, 1)
            pool.wait_ge(s_iota, 2)
            pool.dma_start(place_tab.rearrange("(p c) o -> p (c o)", p=P), place_init[:, :]).then_inc(s_tab, 16)
            pool.wait_ge(s_tab, 16)

            def scatter_places(index, value, ready):
                nc.gpsimd.indirect_dma_start(
                    out=place_tab, out_offset=bass.IndirectOffsetOnAxis(ap=index, axis=0),
                    in_=value, in_offset=None, bounds_check=N - 1, oob_is_err=False).then_inc(ready, 16)

            def turn_places(i):
                pool_wait(p_turn, 16 * i)
                nc.gpsimd.tensor_copy(turn_idx[:, :], last_idx[:, bass.ds(i, 1)]).then_inc(p_tidx, 1)
                nc.gpsimd.tensor_copy(turn_val[:, :], slot_row[:, bass.ds(i, 1)]).then_inc(p_tidx, 1)
                pool_wait(p_tidx, 2 * i + 2)
                scatter_places(turn_idx[:, :], turn_val[:, :], p_turn)

            def other_places(i):
                for u in range(2):
                    at = bass.ds(TURNS + (2 * i + u) * PLACES, PLACES)
                    pool_wait(p_sc[u], 16 * PLACES * i)
                    order.mark(nc.gpsimd.tensor_copy(place_idx[u][:, :], last_idx[:, at]))
                    order.mark(nc.gpsimd.tensor_copy(place_val[u][:, :], slot_row[:, at]))
                    pool_wait(p_copy, order.base + order.k)
                    for j in range(PLACES):
                        scatter_places(place_idx[u][:, j:j + 1], place_val[u][:, j:j + 1], p_sc[u])

            def gather_x(place, k):
                g, u, i = place
                if g is not None:
                    if k == 0:
                        pool_wait(a_st[u], 64 * i)
                        nc.gpsimd.tensor_copy(pool_idx[u][:, 0:G], src_i[:, bass.ds(g * G, G)]).then_inc(p_aidx, 1)
                        nc.gpsimd.tensor_copy(pool_idx[u][:, G:2 * G], dstg_i[:, bass.ds(g * G, G)]).then_inc(p_aidx, 1)
                        pool_wait(p_aidx, 2 * g + 2)
                    for j in range(G):
                        nc.gpsimd.indirect_dma_start(
                            out=xg[u][:, k, j, :], out_offset=None, in_=x,
                            in_offset=bass.IndirectOffsetOnAxis(ap=pool_idx[u][:, k * G + j:k * G + j + 1], axis=0))\
                            .then_inc(a_x[u], 16)

            def add_h(unit, l):
                u, v, _ = unit
                if in_range(u):
                    pool_wait(n_r[l], u + 1)
                    done(pool, n_tb[l], u - 2)
                    nc.gpsimd.tensor_tensor(hT[l + 1][v][:, :], rT[l][:, :], hT[l][v][:, :], ALU.add).then_inc(n_a[l], 1)

            def add_x1(unit):
                u, v, i = unit
                if in_range(u):
                    pool_wait(n_rows[1], u + 1)
                    pool_wait(n_st[3][v], 16 * i)
                    nc.gpsimd.tensor_tensor(flat(on[v]), flat(h2n[v]), flat(x1n[v]), ALU.add).then_inc(n_sum, 1)

            def step(k, v, i):
                at, group = places(k, v, i)
                gather_x(group(-1), 0)
                add_x1(at(0))
                gather_x(group(-1), 1)
                add_h(at(1), 1)
                if v == 1 and not (isinstance(k, int) and k < 0):
                    if isinstance(k, int) and k == 1:
                        pool.wait_ge(s_idx, 1)
                    turn_places(i)

            streams(pool, step)
            turns(pool, other_places, L_TURNS, order)
            for u in range(2):
                pool.wait_ge(p_sc[u], 16 * PLACES * L_TURNS)
            pool.wait_ge(p_turn, 16 * TURNS)

            def take_rows(g, u, i):
                pool_wait(p_ga[u], 16 * G * (i + 1))
                order.mark(nc.gpsimd.tensor_copy(src_row[:, bass.ds(g * G, G)], pool_val[u][:, :]))

            def gather_place(i):
                for u in range(SLOTS_G):
                    g = SLOTS_G * i + u
                    copies(u, g, (pool_idx[u][:, 0:G], src_i))
                    for j in range(G):
                        nc.gpsimd.indirect_dma_start(
                            out=pool_val[u][:, j:j + 1], out_offset=None, in_=place_tab,
                            in_offset=bass.IndirectOffsetOnAxis(ap=pool_idx[u][:, j:j + 1], axis=0)).then_inc(p_ga[u], 16)
                    if u >= 2:
                        take_rows(g - 2, u - 2, i)
                for u in range(2, SLOTS_G):
                    take_rows(SLOTS_G * i + u, u, i)
            turns(pool, gather_place, L_TURNS, order)

            for l in range(LAYERS):
                pool.wait_ge(s_phase, 4 * (2 + l))

                def gather_h(g, u, l=l):
                    pool_wait(e_t, NT * l + G * (g + 1 - SLOTS_G))
                    copies(u, g, (pool_idx[u][:, 0:G], src_row))
                    for j in range(G):
                        nc.gpsimd.indirect_dma_start(
                            out=hsrc[u][:, j, :], out_offset=None, in_=h_tab[l],
                            in_offset=bass.IndirectOffsetOnAxis(ap=pool_idx[u][:, j:j + 1], axis=0)).then_inc(e_hs[u], 16)

                def scatter_out(g, u, i):
                    pool_wait(e_sc[u], 16 * G * i)
                    nc.gpsimd.tensor_copy(pool_val[u][:, :], last_idx[:, bass.ds(g * G, G)]).then_inc(e_oidx, 1)
                    pool_wait(e_oidx, g + 1)
                    pool_wait(e_out, GROUPS * (LAYERS - 1) + g + 1)
                    for j in range(G):
                        nc.gpsimd.indirect_dma_start(
                            out=out, out_offset=bass.IndirectOffsetOnAxis(ap=pool_val[u][:, j:j + 1], axis=0),
                            in_=hnew[u][:, j, :], in_offset=None, bounds_check=N - 1, oob_is_err=False).then_inc(e_sc[u], 16)

                def layer_turn(i, l=l):
                    for u in range(SLOTS_G):
                        g = SLOTS_G * i + u
                        if not (isinstance(g, int) and g + SLOTS_G - 1 >= GROUPS):
                            gather_h(g + SLOTS_G - 1, (u - 1) % SLOTS_G)
                        if l == LAYERS - 1 and not (isinstance(g, int) and g == 0):
                            scatter_out(g - 1, (u - 1) % SLOTS_G, i if u else i - 1)
                for u in range(SLOTS_G - 1):
                    gather_h(u, u)
                turns(pool, layer_turn, L_TURNS, order, head=2)
            scatter_out(GROUPS - 1, SLOTS_G - 1, L_TURNS - 1)
            for u in range(SLOTS_G):
                pool.wait_ge(e_sc[u], 16 * G * L_TURNS)

        @block.scalar
        def _(act):
            act.wait_ge(s_setup, 1)

            def relu_rows(out_rows, in_rows, norm):
                for j in range(norm.n):
                    last = nc.scalar.activation(out_rows[:, j, :], in_rows[:, j, :], ACT.Relu,
                                                bias=norm.shift[:, j:j + 1], scale=norm.rstd[:, j:j + 1])
                return last

            def root(norm, var_ready, count, ready):
                act.wait_ge(var_ready, count)
                nc.scalar.activation(norm.std[:, :], norm.sums[:, 4, :], ACT.Sqrt, bias=eps[:, :], scale=1.0 / D).then_inc(ready, 1)

            def first_root(unit):
                if in_range(unit[0]):
                    root(norm1, n_var1, unit[0] + 1, n_std1)

            def second_root(unit):
                if in_range(unit[0]):
                    root(norm2, n_var2, unit[0] + 1, n_std2)

            def edge_root(place):
                if place[0] is not None:
                    root(norm_e, a_var, place[0] + 1, a_std)

            def relu_h(unit):
                u = unit[0]
                if in_range(u):
                    act.wait_ge(n_t, u + 1)
                    wait(act, n_m, u)
                    nc.scalar.activation(hnT[:, :], psum[4], ACT.Relu).then_inc(n_ht, 1)

            def relu_h0(unit):
                u, v, i = unit
                if in_range(u):
                    act.wait_ge(n_rs2, u + 1)
                    wait(act, n_st[0][v], 16 * i)
                    relu_rows(h0n[v], x1n[v], norm2).then_inc(n_h0, 1)

            def copy_h0t(unit):
                u, v, _ = unit
                if in_range(u):
                    act.wait_ge(n_t0, u + 1)
                    done(act, n_a[0], u - 2)
                    nc.scalar.copy(hT[0][v][:, :], psum[2]).then_inc(n_h0t, 1)

            def relu_bias(unit, l, bank):
                u = unit[0]
                if in_range(u):
                    act.wait_ge(n_z[l], u + 1)
                    wait(act, n_a[l], u)
                    nc.scalar.activation(rT[l][:, :], psum[bank], ACT.Relu, bias=bias_col[:, l:l + 1]).then_inc(n_r[l], 1)

            def copy_rows(unit, l, bank, rows):
                u, v, i = unit
                if in_range(u):
                    act.wait_ge(n_tb[l], u + 1)
                    wait(act, n_st[1 + l][v], 16 * i)
                    if l == 1:
                        done(act, n_sum, u - 2)
                    nc.scalar.copy(flat(rows[v]), psum[bank]).then_inc(n_rows[l], 1)

            def edge_relu(place):
                g, u, _ = place
                if g is not None:
                    act.wait_ge(a_rs, g + 1)
                    wait(act, a_t, g - 1)
                    relu_rows(ah[u], xg[u][:, :, :, :].rearrange("p k j f -> p (k j) f"), norm_e).then_inc(a_h, 1)

            def edge_turned(place):
                g, u, _ = place
                if g is not None:
                    act.wait_ge(a_t, g + 1)
                    wait(act, a_m, g - 1)
                    for c in range(2):
                        last = nc.scalar.copy(flat(ahT[u][:, c * G:(c + 1) * G, :]), psum[5 + c][:, 0:G * P])
                    last.then_inc(a_ht, 1)

            def edge_product(place):
                g, u, i = place
                if g is not None:
                    act.wait_ge(a_m, g + 1)
                    wait(act, a_st[u], 64 * i)
                    wait(act, a_al, g - 1)
                    for c in range(2):
                        last = nc.scalar.copy(flat(e0[u][:, c, :, :]), psum[5 + c][:, 0:G * W0])
                    last.then_inc(a_e0, 1)

            def step(k, v, i):
                at, group = places(k, v, i)
                edge_turned(group(1))
                copy_rows(at(0), 1, 2, h2n)
                first_root(at(4))
                relu_h0(at(2))
                edge_product(group(1))
                relu_bias(at(1), 1, 7)
                edge_root(group(0))
                copy_h0t(at(2))
                copy_rows(at(1), 0, 3, h1n)
                edge_relu(group(0))
                second_root(at(3))
                relu_bias(at(2), 0, 1)
                relu_h(at(4))

            streams(act, step)
            phase_end(act, 1)

            act.wait_ge(m_t, 7)
            nc.scalar.activation(logit[:, 0:NT * HEADS], logit[:, 0:NT * HEADS], ACT.Exp)
            nc.scalar.activation(own[:, :], own[:, :], ACT.Exp).then_inc(m_exp, 1)

            def plain(g, u, i):
                act.wait_ge(b_ld[u], 32 * (i + 1))
                wait(act, b_seg, G * (g - 1))
                nc.scalar.copy(msg0[u % 2][:, :, D:2 * D], l0[u][:, :, 0:D]).then_inc(b_plain, 1)

            def carry(g, u, j):
                if j == 0:
                    act.wait_ge(b_msg, g + 1)
                    act.wait_ge(b_plain, g + 1)
                if j == 0 and isinstance(g, int) and g == 0:
                    held = zeros[:, :]
                else:
                    act.wait_ge(b_seg, G * g + j)
                    held = psum[(G * u + j - 1) % UG][0:1, 0:SEG]
                nc.scalar.copy(msg0[u % 2][0:1, j, :], held).then_inc(b_carry, 1)

            def norm_relu(g, u, i):
                act.wait_ge(b_rs, g + 1)
                wait(act, b_st[u], 32 * i)
                relu_rows(hnew[u], x1e[u], norm_b[u % 2]).then_inc(b_h, 1)

            def b_body(i):
                for u in range(SLOTS_G):
                    g, behind = SLOTS_G * i + u, (u + 1) % SLOTS_G
                    last = isinstance(g, int) and g + 1 >= GROUPS
                    for j in range(1, G):
                        carry(g, u, j)
                        if j == 1 and not last:
                            plain(g + 1, behind, i + (u + 1) // SLOTS_G)
                    if not (isinstance(g, int) and g < 2):
                        norm_relu(g - 2, (u - 2) % SLOTS_G, i + (u - 2) // SLOTS_G)
                    if not (isinstance(g, int) and g == 0):
                        root(norm_b[(u - 1) % 2], b_var, g, b_std)
                    if not last:
                        carry(g + 1, behind, 0)
            plain(0, 0, 0)
            carry(0, 0, 0)
            turns(act, b_body, L_TURNS, head=2)
            root(norm_b[(GROUPS - 1) % 2], b_var, GROUPS, b_std)
            for k in (2, 1):
                norm_relu(GROUPS - k, SLOTS_G - k, L_TURNS - 1)
            phase_end(act, 2)

            for l in range(LAYERS):
                def turned(i, j, l=l):
                    i, j = i + j // LG, j % LG
                    if isinstance(i, int) and i >= L_TURNS:
                        return
                    t = NT * l + LG * i + j
                    act.wait_ge(e_t, t + 1)
                    wait(act, e_seg, t - UG + 1)
                    nc.scalar.copy(pairT[j % UG][:, 1:], psum[j % 2][:, 1:2 * P]).then_inc(e_ct, 1)

                def first_term(i, j, l=l):
                    i, j = i + j // LG, j % LG
                    if isinstance(i, int) and i >= L_TURNS:
                        return
                    t = NT * l + LG * i + j
                    act.wait_ge(e_y, t + 1)
                    wait(act, e_seg, t - UG + 1)
                    nc.scalar.activation(msg[j % UG][:, :], psum[2 + j % 3][:, 0:D], ACT.Copy,
                                         scale=coef[:, l, bass.ds(LG * i + j, 1), 0]).then_inc(e_first, 1)

                def e_body(i, l=l):
                    for j in range(LG):
                        t = NT * l + LG * i + j
                        act.wait_ge(e_msg, t + 1)
                        if isinstance(i, int) and i == 0 and j == 0:
                            held = zeros[:, 0:D]
                        else:
                            act.wait_ge(e_seg, t)
                            b = (j - 1) % UG
                            held = psum[5 + b // G][0:1, (b % G) * D:(b % G + 1) * D]
                        nc.scalar.copy(msg[j % UG][0:1, :], held).then_inc(e_carry, 1)
                        turned(i, j + 3)
                        first_term(i, j + 2)
                for j in range(3):
                    turned(0, j)
                act.wait_ge(s_coef, l + 1)
                for j in range(2):
                    first_term(0, j)
                turns(act, e_body, L_TURNS)
                phase_end(act, 3 + l)

        @block.vector
        def _(dve):
            order = Order(dve, s_order)
            nc.vector.memset(zeros[:, :], 0.0)
            nc.vector.memset(ones[:, :], 1.0)
            nc.vector.memset(eps[:, :], EPS).then_inc(s_setup, 1)
            dve.wait_ge(s_const, 16 * CONSTS)
            for k in range(2):
                last = nc.vector.tensor_scalar(att_mat[:, k * HEADS:(k + 1) * HEADS], headmask[:, :], att_cols[:, k:k + 1],
                                               None, ALU.mult)
            last.then_inc(s_setup, 1)
            dve.wait_ge(s_wt, 1)
            nc.vector.tensor_copy(w0[:, :], psum[0][:, 0:W0]).then_inc(s_w0, 1)
            nc.vector.memset(logit[:, :], 0.0)
            for k in range(UG):
                nc.vector.memset(pairT[k][:, 0:1], 0.0)
            dve.wait_ge(s_later, 16 * LATER_CONSTS)
            order.mark(nc.vector.tensor_tensor(repeat_f[:, :], dst_i[:, :], next_i[:, :], ALU.is_equal))
            nc.vector.tensor_copy(dst_f[:, :], dst_i[:, :])
            nc.vector.tensor_copy(ends_f[:, :, 0], scan_i[:, :, P - 1])
            nc.vector.tensor_copy(ends_f[:, :, 1], scan_i[:, :, 1])
            for r in range(REL):
                last = nc.vector.tensor_single_scalar(is_r[:, r, :], etype_i[:, :], float(r), ALU.is_equal)
            order.mark(last)
            order.wait()
            nc.vector.scalar_tensor_tensor(out=last_idx[:, :], in0=repeat_f[:, :], scalar=float(SKIP), in1=dst_i[:, :],
                                           op0=ALU.mult, op1=ALU.add).then_inc(s_idx, 1)

            def make_coef(l):
                for r in range(REL):
                    for b in range(BASES):
                        c = comb_bc[:, l, r, b:b + 1]
                        if r == 0:
                            last = nc.vector.tensor_scalar(coef[:, l, :, b], is_r[:, r, :], c, None, ALU.mult)
                        else:
                            last = nc.vector.scalar_tensor_tensor(out=coef[:, l, :, b], in0=is_r[:, r, :], scalar=c,
                                                                  in1=coef[:, l, :, b], op0=ALU.mult, op1=ALU.add)
                    if r < REL - 1:
                        order.mark(last)
                        order.wait()
                last.then_inc(s_coef, 1)
                dve.wait_ge(s_coef, l + 1)

            def bn(rows, norm):
                for j in range(norm.n):
                    last = nc.vector.bn_stats(norm.stats[:, j, :], rows[:, j, :])
                order.mark(last)

            def first_stats(unit):
                u, v, i = unit
                if in_range(u):
                    dve.wait_ge(n_x[v], 16 * (i + 1))
                    wait(dve, n_rs1, u)
                    bn(xn[v], norm1)
                    variance(order, norm1, n_var1)

            def first_scale(unit):
                if in_range(unit[0]):
                    wait(dve, n_h, unit[0])
                    norm_scale(dve, order, norm1, n_std1, unit[0] + 1, n_rs1)

            def first_norm(unit):
                u, v, _ = unit
                if in_range(u):
                    dve.wait_ge(n_rs1, u + 1)
                    wait(dve, n_t, u)
                    for j in range(J):
                        last = nc.vector.tensor_scalar(hn[:, j, :], xn[v][:, j, :], norm1.rstd[:, j:j + 1], norm1.shift[:, j:j + 1],
                                                       ALU.mult, ALU.add)
                    last.then_inc(n_h, 1)

            def add_h(unit, l):
                u, v, _ = unit
                if in_range(u):
                    dve.wait_ge(n_r[l], u + 1)
                    done(dve, n_z[1], u - 2)
                    nc.vector.tensor_tensor(hT[l + 1][v][:, :], rT[l][:, :], hT[l][v][:, :], ALU.add).then_inc(n_a[l], 1)

            def add_product(unit):
                u, v, _ = unit
                if in_range(u):
                    dve.wait_ge(n_m, u + 1)
                    done(dve, n_sum, u - 2)
                    nc.vector.scalar_tensor_tensor(out=flat(x1n[v]), in0=psum[4], scalar=2.0, in1=flat(xn[v]),
                                                   op0=ALU.mult, op1=ALU.add).then_inc(n_x1, 1)

            def second_stats(unit):
                u, v, _ = unit
                if in_range(u):
                    dve.wait_ge(n_x1, u + 1)
                    wait(dve, n_rs2, u)
                    bn(x1n[v], norm2)
                    variance(order, norm2, n_var2)

            def second_scale(unit):
                if in_range(unit[0]):
                    wait(dve, n_h0, unit[0])
                    norm_scale(dve, order, norm2, n_std2, unit[0] + 1, n_rs2)

            def put_out(unit):
                u, v, _ = unit
                if in_range(u):
                    dve.wait_ge(n_z[2], u + 1)
                    dve.wait_ge(n_sum, u + 1)
                    nc.vector.scalar_tensor_tensor(out=flat(on[v]), in0=psum[0], scalar=0.0, in1=flat(on[v]),
                                                   op0=ALU.max, op1=ALU.add).then_inc(n_out, 1)

            def edge_stats(place):
                g, u, i = place
                if g is not None:
                    dve.wait_ge(a_x[u], 16 * 2 * G * (i + 1))
                    wait(dve, a_rs, g)
                    bn(xg[u][:, :, :, :].rearrange("p k j f -> p (k j) f"), norm_e)
                    variance(order, norm_e, a_var)

            def edge_scale(place):
                g = place[0]
                if g is not None:
                    wait(dve, a_h, g)
                    norm_scale(dve, order, norm_e, a_std, g + 1, a_rs)

            def edge_same(place):
                g, u, i = place
                if g is not None:
                    dve.wait_ge(a_col[u], 16 * (i + 1))
                    wait(dve, a_st[u], 64 * i)
                    for j in range(G):
                        last = nc.vector.tensor_scalar(same[u][:, j, :], col_i[u][:, j, :], dst_f[:, bass.ds(g * G + j, 1)],
                                                       None, ALU.is_equal)
                    last.then_inc(a_same, 1)

            def edge_logits(place):
                g, u, _ = place
                if g is not None:
                    dve.wait_ge(a_e0, g + 1)
                    to = bass.ds(g * (G * HEADS), G * HEADS)
                    a_src, a_own, a_dst = e0[u][:, 0, :, D:D + HEADS], e0[u][:, 1, :, D:D + HEADS], e0[u][:, 1, :, D + HEADS:W0]
                    nc.vector.tensor_tensor(logit[:, to].rearrange("p (g h) -> p g h", h=HEADS), a_src, a_dst, ALU.add)
                    nc.vector.tensor_tensor(own[:, to].rearrange("p (g h) -> p g h", h=HEADS), a_own, a_dst, ALU.add).then_inc(a_al, 1)

            def step(k, v, i):
                at, group = places(k, v, i)
                second_scale(at(2))
                first_stats(at(4))
                add_h(at(1), 0)
                edge_stats(group(0))
                edge_same(group(1))
                first_scale(at(4))
                add_product(at(3))
                edge_scale(group(0))
                second_stats(at(3))
                first_norm(at(4))
                edge_logits(group(1))
                put_out(at(0))

            streams(dve, step, order)
            phase_end(dve, 1)

            n_log = NT * HEADS
            order.mark(nc.vector.scalar_tensor_tensor(out=logit[:, 0:n_log], in0=logit[:, 0:n_log], scalar=SLOPE,
                                                      in1=logit[:, 0:n_log], op0=ALU.mult, op1=ALU.max))
            order.mark(nc.vector.scalar_tensor_tensor(out=own[:, :], in0=own[:, :], scalar=SLOPE, in1=own[:, :],
                                                      op0=ALU.mult, op1=ALU.max))
            order.wait()
            nc.vector.memset(logit[0:1, :], -BIG).then_inc(m_t, 1)
            dve.wait_ge(m_pe, 1)
            nc.vector.tensor_copy(flat(best)[:, 0:512], psum[0])
            order.mark(nc.vector.tensor_copy(flat(best)[:, 512:BLOCKS * P], psum[1][:, 0:BLOCKS * P - 512]))
            d = 1
            while d < P:
                order.wait()
                order.mark(nc.vector.tensor_tensor(differ[:, :, 0:P - d], scan_i[:, :, 0:P - d], scan_i[:, :, d:P], ALU.not_equal))
                order.wait()
                nc.vector.scalar_tensor_tensor(out=up[:, :, 0:P - d], in0=differ[:, :, 0:P - d], scalar=-BIG,
                                               in1=best[:, :, d:P], op0=ALU.mult, op1=ALU.add)
                order.mark(nc.vector.scalar_tensor_tensor(out=down[:, :, 0:P - d], in0=differ[:, :, 0:P - d], scalar=-BIG,
                                                          in1=best[:, :, 0:P - d], op0=ALU.mult, op1=ALU.add))
                order.wait()
                order.mark(nc.vector.tensor_tensor(best[:, :, 0:P - d], best[:, :, 0:P - d], up[:, :, 0:P - d], ALU.max))
                order.wait()
                order.mark(nc.vector.tensor_tensor(best[:, :, d:P], best[:, :, d:P], down[:, :, 0:P - d], ALU.max))
                d *= 2
            order.wait()
            for k, c in enumerate((P - 1, 1)):
                last = nc.vector.tensor_tensor(edge_max[:, k, :, :], tilesel[:, :].unsqueeze(1).broadcast_to([P, BLOCKS, 32]),
                                               best[:, :, c:c + 1].broadcast_to([P, BLOCKS, 32]), ALU.mult)
            last.then_inc(m_t, 1)
            dve.wait_ge(m_pe, 2)
            for k in range(2):
                order.wait()
                for b in range(BLOCKS):
                    last = nc.vector.tensor_scalar(pick[:, b, :], ends_i[:, k, :], ends_f[:, b, 1 - k:2 - k], -BIG,
                                                   ALU.not_equal, ALU.mult)
                order.mark(last)
                order.wait()
                order.mark(nc.vector.tensor_tensor(pick[:, :, :], pick[:, :, :],
                                                   psum[2 + k][:, 0:BLOCKS * 32].unsqueeze(1).broadcast_to([P, BLOCKS, BLOCKS * 32]), ALU.add))
                order.wait()
                order.mark(nc.vector.tensor_reduce(beyond[:, k, :], pick[:, :, :], AX.X, ALU.max))
                order.mark(nc.vector.tensor_tensor(differ[:, :, :], scan_i[:, :, :],
                                                   ends_f[:, :, 1 - k:2 - k].broadcast_to([P, BLOCKS, P]), ALU.not_equal))
                order.wait()
                order.mark(nc.vector.scalar_tensor_tensor(out=up[:, :, :], in0=differ[:, :, :], scalar=-BIG,
                                                          in1=beyond[:, k, :].unsqueeze(2).broadcast_to([P, BLOCKS, P]),
                                                          op0=ALU.mult, op1=ALU.add))
                order.wait()
                ins = nc.vector.tensor_tensor(best[:, :, :], best[:, :, :], up[:, :, :], ALU.max)
                order.mark(ins)
            order.wait()
            nc.vector.tensor_copy(down[:, :, :], best[:, :, :]).then_inc(m_t, 1)
            dve.wait_ge(m_pe, 3)
            nc.vector.tensor_tensor(top[:, 0:512], psum[0][:, :], own[:, 0:512], ALU.max)
            order.mark(nc.vector.tensor_tensor(top[:, 512:n_log], psum[1][:, 0:n_log - 512], own[:, 512:n_log], ALU.max))
            order.wait()
            nc.vector.tensor_tensor(logit[:, 0:n_log], logit[:, 0:n_log], top[:, :], ALU.subtract).then_inc(m_t, 2)
            nc.vector.tensor_tensor(own[:, :], own[:, :], top[:, :], ALU.subtract).then_inc(m_t, 2)
            dve.wait_ge(m_exp, 1)

            def weigh(g, u, i):
                w = logit[:, bass.ds(g * (G * HEADS), G * HEADS)].rearrange("p (g h) -> p g h", h=HEADS)
                dve.wait_ge(b_ld[u], 32 * (i + 1))
                wait(dve, b_seg, G * (g - 1))
                nc.vector.tensor_tensor(heads(msg0[u % 2][:, :, 0:D]), heads(l0[u][:, :, 0:D]), per_head(w), ALU.mult)
                nc.vector.tensor_copy(msg0[u % 2][:, :, 2 * D:SEG], w).then_inc(b_msg, 1)
                nc.vector.tensor_tensor(t_sum[u % 2][:, :, :], l0[u][:, :, D:2 * D], l0[u][:, :, 2 * D:3 * D], ALU.add).then_inc(b_plus, 1)

            def b_body(i):
                for u in range(SLOTS_G):
                    g, w = SLOTS_G * i + u, u % 2
                    w_own = own[:, bass.ds(g * (G * HEADS), G * HEADS)].rearrange("p (g h) -> p g h", h=HEADS)
                    if not (isinstance(g, int) and g + 1 >= GROUPS):
                        weigh(g + 1, (u + 1) % SLOTS_G, i + (u + 1) // SLOTS_G)
                        dve.wait_ge(b_carry, G * (g + 1) + 1)
                    dve.wait_ge(b_seg, G * (g + 1))
                    sums = banks[:, G * w:G * (w + 1), :]
                    ins = nc.vector.tensor_tensor(den[:, :, :], sums[:, :, 2 * D:SEG], w_own, ALU.add)
                    ins.then_inc(b_den, 1)
                    dve.wait_ge(b_plus, g + 1)
                    nc.vector.tensor_tensor(t_nbr[:, :, :], t_sum[w][:, :, :], sums[:, :, D:2 * D], ALU.add).then_inc(b_nbr, 1)
                    dve.wait_ge(b_den, g + 1)
                    nc.vector.reciprocal(rden[:, :, :], den[:, :, :]).then_inc(b_rden, 1)
                    if not (isinstance(g, int) and g == 0):
                        scale_first(g - 1, 1 - w)
                    dve.wait_ge(b_rden, g + 1)
                    nc.vector.tensor_tensor(pself[:, :, :], w_own, rden[:, :, :], ALU.mult).then_inc(b_pself, 1)
                    nc.vector.tensor_tensor(heads(t_att[:, :, :]), heads(sums[:, :, 0:D]), per_head(rden[:, :, :]), ALU.mult)\
                        .then_inc(b_att, 1)
                    dve.wait_ge(b_pself, g + 1)
                    nc.vector.tensor_tensor(heads(t_own[:, :, :]), heads(l0[u][:, :, D:2 * D]), per_head(pself[:, :, :]), ALU.mult)\
                        .then_inc(b_own, 1)
                    dve.wait_ge(b_att, g + 1)
                    nc.vector.tensor_tensor(t_nbr[:, :, :], t_nbr[:, :, :], t_att[:, :, :], ALU.add).then_inc(b_nbr, 1)
                    if not (isinstance(g, int) and g == 0):
                        scale_second(g - 1, 1 - w)
                    dve.wait_ge(b_nbr, 2 * g + 2)
                    wait(dve, b_st[u], 32 * i)
                    nc.vector.tensor_tensor(x1e[u][:, :, :], t_own[:, :, :], t_nbr[:, :, :], ALU.add).then_inc(b_x1, 1)
                    dve.wait_ge(b_x1, g + 1)
                    for j in range(G):
                        last = nc.vector.bn_stats(norm_b[w].stats[:, j, :], x1e[u][:, j, :])
                    last.then_inc(b_bn, 1)
                    st, (total, half, m2, sq, var) = norm_b[w].stats, (norm_b[w].sums[:, c, :] for c in range(5))
                    dve.wait_ge(b_bn, g + 1)
                    nc.vector.tensor_tensor(half, st[:, :, 1], st[:, :, 4], ALU.subtract).then_inc(b_half, 1)
                    nc.vector.tensor_tensor(m2, st[:, :, 2], st[:, :, 5], ALU.add)
                    dve.wait_ge(b_half, g + 1)
                    nc.vector.tensor_tensor(sq, half, half, ALU.mult).then_inc(b_sq, 1)
                    nc.vector.tensor_tensor(total, st[:, :, 1], st[:, :, 4], ALU.add)
                    dve.wait_ge(b_sq, g + 1)
                    nc.vector.scalar_tensor_tensor(out=var, in0=sq, scalar=D / 4.0, in1=m2, op0=ALU.mult, op1=ALU.add).then_inc(b_var, 1)

            def scale_first(g, u):
                dve.wait_ge(b_std, g + 1)
                wait(dve, b_h, g - 1)
                nc.vector.reciprocal(norm_b[u].rstd[:, :], norm_b[u].std[:, :]).then_inc(b_rstd, 1)

            def scale_second(g, u):
                dve.wait_ge(b_rstd, g + 1)
                nc.vector.scalar_tensor_tensor(out=norm_b[u].shift[:, :], in0=norm_b[u].sums[:, 0, :], scalar=-0.5,
                                               in1=norm_b[u].rstd[:, :], op0=ALU.mult, op1=ALU.mult).then_inc(b_rs, 1)
            weigh(0, 0, 0)
            turns(dve, b_body, L_TURNS)
            scale_first(GROUPS - 1, 1)
            scale_second(GROUPS - 1, 1)
            phase_end(dve, 2)

            for l in range(LAYERS):
                def term(i, j, b, l=l):
                    i, j = i + j // LG, j % LG
                    if isinstance(i, int) and i >= L_TURNS:
                        return
                    t = NT * l + LG * i + j
                    if b == 1:
                        dve.wait_ge(e_first, t + 1)
                    else:
                        dve.wait_ge(e_msg1 if b == 2 else e_msg2, t + 1)
                    nc.vector.scalar_tensor_tensor(
                        out=msg[j % UG][:, :], in0=psum[2 + j % 3][:, b * D:(b + 1) * D], scalar=coef[:, l, bass.ds(LG * i + j, 1), b],
                        in1=msg[j % UG][:, :], op0=ALU.mult, op1=ALU.add).then_inc((e_msg1, e_msg2, e_msg)[b - 1], 1)

                def sum_bias(g, u, l=l):
                    dve.wait_ge(e_seg, NT * l + G * (g + 1))
                    wait(dve, e_out, GROUPS * l + g)
                    nc.vector.tensor_tensor(
                        zsum[:, :, :], psum[5 + u % 2][:, 0:G * D].rearrange("p (g f) -> p g f", g=G),
                        bias_row[:, l:l + 1, :].broadcast_to([P, G, D]), ALU.add).then_inc(e_z, 1)

                def relu_add(g, u, i, l=l):
                    dve.wait_ge(e_ld[u], 32 * (L_TURNS * l + i + 1))
                    if l < LAYERS - 1:
                        wait(dve, e_st[u], 16 * (L_TURNS * l + i))
                        to = hnew[u][:, :, :]
                    else:
                        to = zsum[:, :, :]
                    dve.wait_ge(e_z, GROUPS * l + g + 1)
                    ins = nc.vector.scalar_tensor_tensor(
                        out=to.rearrange("p g f -> p (g f)"), in0=zsum[:, :, :].rearrange("p g f -> p (g f)"), scalar=0.0,
                        in1=hdst[u][:, :, :].rearrange("p g f -> p (g f)"), op0=ALU.max, op1=ALU.add)
                    ins.then_inc(e_relu if l == LAYERS - 1 else e_out, 1)

                def add_x1(g, u, i, l=l):
                    if l == LAYERS - 1:
                        dve.wait_ge(e_x1[u], 16 * (i + 1))
                        wait(dve, e_sc[u], 16 * G * i)
                        dve.wait_ge(e_relu, g + 1)
                        nc.vector.tensor_tensor(hnew[u][:, :, :], zsum[:, :, :], x1e[u][:, :, :], ALU.add).then_inc(e_out, 1)

                def e_body(i, l=l):
                    for j in range(LG):
                        u = j // G
                        g = SLOTS_G * i + u
                        put = j % G == 1 and not (isinstance(g, int) and g == 0)
                        term(i, j, 3)
                        term(i, j + 1, 1)
                        if put:
                            dve.wait_ge(e_carry, NT * l + G * g + 1)
                            sum_bias(g - 1, (u - 1) % SLOTS_G)
                        term(i, j + 1, 2)
                        if j % G == 2 and not (isinstance(g, int) and g == 0):
                            relu_add(g - 1, (u - 1) % SLOTS_G, i if u else i - 1)
                            add_x1(g - 1, (u - 1) % SLOTS_G, i if u else i - 1)
                make_coef(l)
                term(0, 0, 1)
                term(0, 0, 2)
                turns(dve, e_body, L_TURNS, head=2)
                sum_bias(GROUPS - 1, SLOTS_G - 1)
                relu_add(GROUPS - 1, SLOTS_G - 1, L_TURNS - 1)
                add_x1(GROUPS - 1, SLOTS_G - 1, L_TURNS - 1)
                phase_end(dve, 3 + l)

        @block.tensor
        def _(pe):
            pe.wait_ge(s_const, 16 * CONSTS)
            pe.wait_ge(s_setup, 2)
            nc.tensor.transpose(psum[0][:, 0:D], w_rows[:, :], ident[:, :])
            nc.tensor.matmul(psum[0][:, D:W0], w_rows[:, :], att_mat[:, :], start=True, stop=True).then_inc(s_wt, 1)
            pe.wait_ge(s_w0, 1)

            def turn(bank, blocks, n):
                for j in range(n):
                    last = nc.tensor.transpose(psum[bank][:, j * P:(j + 1) * P], blocks(j), ident[:, :])
                return last

            def turn_h(unit):
                u = unit[0]
                if in_range(u):
                    pe.wait_ge(n_h, u + 1)
                    turn(4, lambda j: hn[:, j, :], J).then_inc(n_t, 1)

            def product(unit):
                u = unit[0]
                if in_range(u):
                    pe.wait_ge(n_ht, u + 1)
                    for j in range(J):
                        last = nc.tensor.matmul(psum[4][:, j * D:(j + 1) * D], hnT[:, j * P:(j + 1) * P], w0[:, 0:D],
                                                start=True, stop=True)
                    last.then_inc(n_m, 1)

            def turn_h0(unit):
                u, v, _ = unit
                if in_range(u):
                    pe.wait_ge(n_h0, u + 1)
                    turn(2, lambda j: h0n[v][:, j, :], J).then_inc(n_t0, 1)

            def through(unit, l, bank, ready):
                u, v, _ = unit
                if in_range(u):
                    pe.wait_ge(ready, u + 1)
                    nc.tensor.matmul(psum[bank], wl[:, l, :], hT[l][v][:, :], start=True, stop=True).then_inc(n_z[l], 1)

            def turned_back(unit, l, bank):
                u, v, _ = unit
                if in_range(u):
                    pe.wait_ge(n_a[l], u + 1)
                    turn(bank, lambda j: hT[l + 1][v][:, j * P:(j + 1) * P], J).then_inc(n_tb[l], 1)

            def last_layer(unit):
                u, v, _ = unit
                if in_range(u):
                    pe.wait_ge(n_a[1], u + 1)
                    for j in range(J):
                        to = psum[0][:, j * D:(j + 1) * D]
                        nc.tensor.matmul(to, hT[2][v][:, j * P:(j + 1) * P], wl[:, 2, :], start=True, stop=False)
                        last = nc.tensor.matmul(to, ones[:, :], bias_row[0:1, 2, :], start=False, stop=True)
                    last.then_inc(n_z[2], 1)

            def edge_turn(place):
                g, u, _ = place
                if g is not None:
                    pe.wait_ge(a_h, g + 1)
                    wait(pe, a_e0, g)
                    for c in range(2):
                        last = turn(5 + c, lambda j: ah[u][:, c * G + j, :], G)
                    last.then_inc(a_t, 1)

            def edge_products(place):
                g, u, _ = place
                if g is not None:
                    pe.wait_ge(a_ht, g + 1)
                    for c in range(2):
                        for j in range(G):
                            last = nc.tensor.matmul(psum[5 + c][:, j * W0:(j + 1) * W0], ahT[u][:, c * G + j, :], w0[:, :],
                                                    start=True, stop=True)
                    last.then_inc(a_m, 1)

            def step(k, v, i):
                at, group = places(k, v, i)
                done(pe, n_x1, k + 3)
                turn_h(at(3))
                edge_turn(group(1))
                done(pe, n_h0t, k + 2)
                turned_back(at(0), 1, 2)
                done(pe, n_ht, k + 4)
                product(at(3))
                edge_products(group(1))
                done(pe, n_r[1], k + 1)
                through(at(1), 1, 7, n_a[0])
                done(pe, n_rows[0], k + 1)
                turned_back(at(1), 0, 3)
                done(pe, n_rows[1], k + 1)
                turn_h0(at(2))
                done(pe, n_out, k)
                last_layer(at(0))
                done(pe, n_r[0], k + 2)
                through(at(2), 0, 1, n_h0t)

            streams(pe, step)
            phase_end(pe, 1)

            pe.wait_ge(m_t, 1)
            for b in range(BLOCKS):
                last = nc.tensor.transpose(psum[b // 4][:, (b % 4) * P:(b % 4 + 1) * P], logit[:, b * P:(b + 1) * P], ident[:, :])
            last.then_inc(m_pe, 1)
            pe.wait_ge(m_t, 2)
            for k in range(2):
                last = nc.tensor.matmul(psum[2 + k][:, 0:BLOCKS * 32], headsel[:, :], edge_max[:, k, :, :].rearrange("p b c -> p (b c)"),
                                        start=True, stop=True)
            last.then_inc(m_pe, 1)
            pe.wait_ge(m_t, 3)
            for b in range(BLOCKS):
                last = nc.tensor.transpose(psum[b // 4][:, (b % 4) * P:(b % 4 + 1) * P], down[:, b, :], ident[:, :])
            last.then_inc(m_pe, 1)

            def b_body(i):
                for u in range(SLOTS_G):
                    g = SLOTS_G * i + u
                    pe.wait_ge(b_ld[u], 32 * (i + 1))
                    wait(pe, b_x1, g - 1)
                    for j in range(G):
                        pe.wait_ge(b_carry, G * g + j + 1)
                        nc.tensor.matmul(psum[G * (u % 2) + j][:, 0:SEG], same[u][:, j, :], msg0[u % 2][:, j, :],
                                         start=True, stop=True).then_inc(b_seg, 1)
            turns(pe, b_body, L_TURNS)
            phase_end(pe, 2)

            for l in range(LAYERS):
                def to_turn(i, j, l=l):
                    i, j = i + j // LG, j % LG
                    if isinstance(i, int) and i >= L_TURNS:
                        return
                    t, u = NT * l + LG * i + j, j // G
                    if j % G == 0:
                        pe.wait_ge(e_hs[u], 16 * G * (L_TURNS * l + i + 1))
                        pe.wait_ge(e_ld[u], 32 * (L_TURNS * l + i + 1))
                    wait(pe, e_ct, t - 1)
                    nc.tensor.transpose(psum[j % 2][:, 0:P], hdst[u][:, j % G, :], ident[:, :])
                    nc.tensor.transpose(psum[j % 2][:, P:2 * P], hsrc[u][:, j % G, :], ident[:, :]).then_inc(e_t, 1)

                def project(i, j, l=l):
                    i, j = i + j // LG, j % LG
                    if isinstance(i, int) and i >= L_TURNS:
                        return
                    t = NT * l + LG * i + j
                    pe.wait_ge(e_ct, t + 1)
                    wait(pe, e_msg, t - 2)
                    nc.tensor.matmul(psum[2 + j % 3][:, :], pairT[j % UG][:, P:2 * P], basis_sb[:, l, :], start=True, stop=True)\
                        .then_inc(e_y, 1)

                def e_body(i, l=l):
                    for j in range(LG):
                        to_turn(i, j + 3)
                        project(i, j + 2)
                        t, u = NT * l + LG * i + j, j // G
                        if j % G == 0:
                            wait(pe, e_z, GROUPS * l + SLOTS_G * i + u - 1)
                        at = psum[5 + u % 2][:, (j % G) * D:(j % G + 1) * D]
                        pe.wait_ge(e_carry, t + 1)
                        nc.tensor.matmul(at, pairT[j % UG][:, 0:P], wl[:, l, :], start=True, stop=False)
                        nc.tensor.matmul(at, same[u][:, j % G, :], msg[j % UG][:, :], start=False, stop=True).then_inc(e_seg, 1)
                for j in range(3):
                    to_turn(0, j)
                for j in range(2):
                    project(0, j)
                turns(pe, e_body, L_TURNS)
                phase_end(pe, 3 + l)


def kernel(**inputs):
    import concourse.bacc as bacc
    from concourse.bass_utils import run_bass_kernel_spmd as run

    a = {k: np.asarray(v) for k, v in inputs.items()}
    src, dst, etype = a["src"], a["dst"], a["edge_type_8"]

    def slots(edge_values, first_column, pad):
        rest = np.full(NT * TE - E, pad, np.int32)
        body = np.concatenate([edge_values.astype(np.int32), rest]).reshape(NT, TE)
        return np.concatenate([first_column.reshape(NT, 1).astype(np.int32), body], axis=1)

    zero = np.zeros(NT, np.int32)
    padded = np.concatenate([dst, np.full(NT * TE - E, NO_EDGE, np.int32)]).reshape(NT, TE)
    ends = padded[:, -1]
    before = np.concatenate([np.full(1, NO_SEGMENT, np.int32), ends[:-1]])
    follow = np.concatenate([dst[1:], np.full(1, NO_SEGMENT, np.int32)])
    dst_slots = slots(dst, before, NO_EDGE)
    all_tiles = np.concatenate([dst_slots, np.full((BLOCKS * 32 - NT, P), NO_EDGE, np.int32)])
    scan = np.repeat(all_tiles.reshape(BLOCKS, 32, 1, P), HEADS, axis=2).transpose(1, 2, 0, 3).reshape(P, BLOCKS * P)
    tile_ends = np.stack([all_tiles[:, P - 1], all_tiles[:, 1]])
    tl, hd = np.arange(P) // HEADS, np.arange(P) % HEADS
    consts = np.concatenate([
        np.eye(P), np.arange(P)[:, None] // HD == np.arange(HEADS)[None, :],
        hd[:, None] == hd[None, :], tl[:, None] == np.arange(32)[None, :]], axis=1).astype(np.float32)
    arrays = {
        "x": a["x"], "src": slots(src, zero, 0).T, "dst_cols": dst_slots.T, "col_dst": slots(dst, ends, NO_EDGE),
        "next_dst": slots(follow, before, NO_EDGE).T, "dst_gather": slots(dst, zero, 0).T,
        "etype": slots(etype, zero, 0).T, "scan_dst": scan, "tile_ends": tile_ends, "consts": consts,
        "W": a["L0_gnn_W"], "att": np.stack([a["L0_gnn_att_src"].reshape(D), a["L0_gnn_att_dst"].reshape(D)], axis=1),
        "basis": a["L1_gnn_basis"], "comb": a["L1_gnn_comb"], "w_loop": a["L1_gnn_w_loop"], "bias": a["L1_gnn_bias"],
    }
    arrays = {f"in_{k}": np.ascontiguousarray(v) for k, v in arrays.items()}
    nc = bacc.Bacc("TRN2", target_bir_lowering=False, num_devices=1)
    aps = [nc.dram_tensor(k, v.shape, mybir.dt.from_np(v.dtype), kind="ExternalInput").ap() for k, v in arrays.items()]
    aps.append(nc.dram_tensor("out", (N, D), mybir.dt.float32, kind="ExternalOutput").ap())
    program(nc, *aps)
    return run(nc, [arrays], core_ids=[0]).results[0]["out"]
```
